# Optimizing a Trainium2 kernel written in Bass

```python
import numpy as np
import jax
import jax.numpy as jnp

def _softmax(x, axis=-1):
    return jax.nn.softmax(x, axis=axis)

def _gelu(x):
    return jax.nn.gelu(x, approximate=True)

def _silu(x):
    return jax.nn.silu(x)

def _sigmoid(x):
    return jax.nn.sigmoid(x)

def _layernorm(x, axis=-1, eps=1e-05):
    m = jnp.mean(x, axis=axis, keepdims=True)
    v = jnp.var(x, axis=axis, keepdims=True)
    return (x - m) / jnp.sqrt(v + eps)

def _scatter_add(tgt, idx, src, axis=0):
    return tgt.at[idx].add(src)

def _segment_sum(src, seg, n):
    return jax.ops.segment_sum(src, seg, n)
kernel_name = 'mk_seq_preln_d1_jaxref_r8_8a84ef'

def setup_inputs(seed: int=0):
    np.random.seed(seed)
    _w = jnp.asarray

    def _L0_attn_setup():
        import jax, jax.numpy as jnp
        import numpy as np
        N_CHANNELS = 128
        N_HEADS = 16
        BLOCK_SIZE = 256
        BATCH = 4
        SEQ = 256
        key = jax.random.key(seed)
        k_x, k_wqkv, k_wproj = jax.random.split(key, 3)
        x = jax.random.normal(k_x, (BATCH, SEQ, N_CHANNELS), dtype=jnp.float32)
        W_qkv = jax.random.normal(k_wqkv, (3 * N_CHANNELS, N_CHANNELS), dtype=jnp.float32) * 0.02
        b_qkv = jnp.zeros((3 * N_CHANNELS,), dtype=jnp.float32)
        W_proj = jax.random.normal(k_wproj, (N_CHANNELS, N_CHANNELS), dtype=jnp.float32) * 0.02
        b_proj = jnp.zeros((N_CHANNELS,), dtype=jnp.float32)
        return {'x': x, 'W_qkv': W_qkv, 'b_qkv': b_qkv, 'W_proj': W_proj, 'b_proj': b_proj}
    _L0_attn_in = _L0_attn_setup()

    def _L0_ffn_setup():
        import jax, jax.numpy as jnp
        import numpy as np
        TOP_K = 2
        LN_EPS = 1e-05
        B, S, H, E, F = (2, 256, 128, 8, 512)

        def _layernorm(x, w, b):
            mu = jnp.mean(x, axis=-1, keepdims=True)
            var = jnp.mean(jnp.square(x - mu), axis=-1, keepdims=True)
            return (x - mu) * jax.lax.rsqrt(var + LN_EPS) * w + b
        key = jax.random.key(seed)
        ks = jax.random.split(key, 6)
        x = jax.random.normal(ks[0], (B, S, H), dtype=jnp.float32)
        Wg = jax.random.normal(ks[1], (H, E), dtype=jnp.float32) * 0.02
        alpha = jax.random.normal(ks[2], (E,), dtype=jnp.float32)
        ln_w = jnp.ones((E, H), dtype=jnp.float32)
        ln_b = jnp.zeros((E, H), dtype=jnp.float32)
        fc1_w = jax.random.normal(ks[3], (E, H, F), dtype=jnp.float32) * 0.02
        fc1_b = jnp.zeros((E, F), dtype=jnp.float32)
        fc2_w = jax.random.normal(ks[4], (E, F, H), dtype=jnp.float32) * 0.02
        fc2_b = jnp.zeros((E, H), dtype=jnp.float32)
        return {'x': x, 'Wg': Wg, 'alpha': alpha, 'ln_w': ln_w, 'ln_b': ln_b, 'fc1_w': fc1_w, 'fc1_b': fc1_b, 'fc2_w': fc2_w, 'fc2_b': fc2_b}
    _L0_ffn_in = _L0_ffn_setup()
    _d = {'L0_attn_x': _L0_attn_in['x'], 'L0_attn_W_qkv': _L0_attn_in['W_qkv'], 'L0_attn_b_qkv': _L0_attn_in['b_qkv'], 'L0_attn_W_proj': _L0_attn_in['W_proj'], 'L0_attn_b_proj': _L0_attn_in['b_proj'], 'L0_ffn_Wg': _L0_ffn_in['Wg'], 'L0_ffn_alpha': _L0_ffn_in['alpha'], 'L0_ffn_ln_w': _L0_ffn_in['ln_w'], 'L0_ffn_ln_b': _L0_ffn_in['ln_b'], 'L0_ffn_fc1_w': _L0_ffn_in['fc1_w'], 'L0_ffn_fc1_b': _L0_ffn_in['fc1_b'], 'L0_ffn_fc2_w': _L0_ffn_in['fc2_w'], 'L0_ffn_fc2_b': _L0_ffn_in['fc2_b']}
    _x0 = _d['L0_attn_x']
    _d['L0_attn_x'] = jax.random.normal(jax.random.fold_in(jax.random.key(seed), 1), (8, 512, 128), dtype=_x0.dtype)
    del _x0
    return _d

def reference(L0_attn_x, L0_attn_W_qkv, L0_attn_b_qkv, L0_attn_W_proj, L0_attn_b_proj, L0_ffn_Wg, L0_ffn_alpha, L0_ffn_ln_w, L0_ffn_ln_b, L0_ffn_fc1_w, L0_ffn_fc1_b, L0_ffn_fc2_w, L0_ffn_fc2_b):

    def _L0_attn_ref(x, W_qkv, b_qkv, W_proj, b_proj):
        import jax, jax.numpy as jnp
        import numpy as np
        N_CHANNELS = 128
        N_HEADS = 16
        BLOCK_SIZE = 256
        BATCH = 4
        SEQ = 256
        bs, n, n_channels = x.shape
        n_heads = N_HEADS
        head_dim = n_channels // n_heads
        scale = head_dim ** (-0.5)
        qkv = x @ W_qkv.T + b_qkv
        qkv = qkv.reshape(bs, n, 3, n_heads, head_dim)
        q, k, v = (qkv[:, :, 0], qkv[:, :, 1], qkv[:, :, 2])
        logits = jnp.einsum('bthc,bshc->bhts', q, k) * scale
        causal = jnp.tril(jnp.ones((n, n), dtype=bool))
        logits = jnp.where(causal[None, None], logits, -jnp.inf)
        attn = jax.nn.softmax(logits, axis=-1)
        output = jnp.einsum('bhts,bshc->bthc', attn, v)
        output = output.reshape(bs, n, n_channels)
        output = output @ W_proj.T + b_proj
        return output

    def _L0_ffn_ref(x, Wg, alpha, ln_w, ln_b, fc1_w, fc1_b, fc2_w, fc2_b):
        import jax, jax.numpy as jnp
        import numpy as np
        TOP_K = 2
        LN_EPS = 1e-05
        B, S, H, E, F = (2, 256, 128, 8, 512)

        def _layernorm(x, w, b):
            mu = jnp.mean(x, axis=-1, keepdims=True)
            var = jnp.mean(jnp.square(x - mu), axis=-1, keepdims=True)
            return (x - mu) * jax.lax.rsqrt(var + LN_EPS) * w + b
        b, s, h = x.shape
        xf = x.reshape(-1, h)
        logits = xf @ Wg
        top_vals, top_idx = jax.lax.top_k(logits, TOP_K)
        gate_score = jax.nn.softmax(top_vals, axis=-1)
        one_hot = jax.nn.one_hot(top_idx, Wg.shape[1], dtype=xf.dtype)
        comb = jnp.einsum('tke,tk->te', one_hot, gate_score) * alpha
        out = jnp.zeros_like(xf)
        for e in range(Wg.shape[1]):
            hdn = _layernorm(xf, ln_w[e], ln_b[e])
            a = jax.nn.gelu(hdn @ fc1_w[e] + fc1_b[e], approximate=True)
            y = a @ fc2_w[e] + fc2_b[e]
            out = out + y * comb[:, e:e + 1]
        return out.reshape(b, s, h)
    x = L0_attn_x
    x = x + _L0_attn_ref(_layernorm(x, axis=-1), L0_attn_W_qkv, L0_attn_b_qkv, L0_attn_W_proj, L0_attn_b_proj)
    x = x + _L0_ffn_ref(_layernorm(x, axis=-1), L0_ffn_Wg, L0_ffn_alpha, L0_ffn_ln_w, L0_ffn_ln_b, L0_ffn_fc1_w, L0_ffn_fc1_b, L0_ffn_fc2_w, L0_ffn_fc2_b)
    return x

_drawn_inputs = setup_inputs


def setup_inputs(seed=0):
    import zlib

    import numpy as np

    out = dict(_drawn_inputs(seed))
    spreads = {'L0_attn_b_qkv': (0.0, 0.293),
     'L0_attn_b_proj': (0.0, 0.1),
     'L0_ffn_ln_w': (1.0, 0.6),
     'L0_ffn_ln_b': (0.0, 2.0),
     'L0_ffn_fc1_b': (0.0, 0.526),
     'L0_ffn_fc2_b': (0.0, 0.1)}
    factors = {'L0_attn_W_qkv': 8.0}
    for name, (base, spread) in spreads.items():
        noise = np.random.default_rng([zlib.crc32(name.encode()), seed]).standard_normal(out[name].shape)
        drawn = base * np.exp(spread * noise) if base else spread * noise
        out[name] = jnp.asarray(drawn.astype(out[name].dtype))
    for name, factor in factors.items():
        out[name] = (out[name] * factor).astype(out[name].dtype)
    return out
```

```python
from contextlib import ExitStack

import numpy as np

import concourse.bass as bass
from concourse import mybir

F32, BF16, U32 = mybir.dt.float32, mybir.dt.bfloat16, mybir.dt.uint32
ALU = mybir.AluOpType
ACT = mybir.ActivationFunctionType
AX = mybir.AxisListType

P = 128
EPS = 1e-5
NEG = -3.0e38
PARTS = 3
Q_PRODUCTS = ((0, 3, 0, 0), (3, 2, 1, 0), (5, 1, 2, 0))
K_PRODUCTS = ((0, 3, 0, 1), (3, 2, 0, 1), (5, 1, 0, 1))
MAX_ROW = 96
K1, K2 = MAX_ROW, MAX_ROW + PARTS
HPG = 4
UNITS = 6
UNIT = ((4, (0, 1)), (4, (2, 3)), (3, (0, 1)), (3, (2, 3)), (2, (0, 1, 2, 3)), (1, (0, 1, 2, 3)))
LAG = 2
PV_LAG = 2
SLOTS = 3
P_RING = 4


def build(nc, x, wqT, wkT, wvT, bq, bk, bv, wpT, bp, wg, alpha, lnwT, lnbT, w1, b1T, w2, b2, out):
    B, T, C = x.shape
    E, F = w1.shape[0], w1.shape[2]
    D = 8
    H = C // D
    NT = T // P
    NG = H // HPG
    G = B * NG
    NK = F // P
    SCALE = float(D) ** -0.5

    extra = {}

    def at(g, u, *stage):
        extra.setdefault((g, u), []).append(stage)

    for b in range(1, B):
        g = NG * (b - 1)
        at(g, 0, "ln_stats", b)
        at(g, 1, "ln_apply", b)
        at(g, 2, "xnT", b)
        at(g, 3, "q", b)
        for i in range(4):
            at(g + (4 + i) // 6, (4 + i) % 6, "split", b, 0, i)
        at(g + 1, 2, "stack", b, 0)
        at(g + 1, 2, "k", b)
        for i in range(4):
            at(g + 1 + (3 + i) // 6, (3 + i) % 6, "split", b, 1, i)
        at(g + 2, 1, "stack", b, 1)
        at(g + 2, 3, "v", b)
    for g in range(G):
        at(g + 1, 1, "maxT", g)
        at(g + 1, 2, "max_parts", g)
        at(g + LAG + 1, 1, "pv_out", g)
        at(g + LAG + 1, 4, "oT", g)
        if g % NG == NG - 1:
            b = g // NG
            at(g + LAG, 0, "residual", b)
            at(g + LAG + 1, 5, "onT", b)
            at(g + LAG + 2, 0, "proj", b)
    at(3, 5, "hidden_bias")
    for e in range(E):
        at(5 + e, 5, "scale_w1", e)
    ROUTE = ("r_stats1", "r_xf", "r_z", "xfT", "zT", "gate", "r_top", "r_comb", "combT", "fc2_bias")
    for i, r in enumerate(ROUTE):
        at(17 + i, 5, r, 0)

    schedule = [("ln_stats", 0), ("ln_apply", 0), ("xnT", 0), ("q", 0)]
    schedule += [("split", 0, 0, i) for i in range(4)] + [("stack", 0, 0), ("k", 0)]
    schedule += [("split", 0, 1, i) for i in range(4)] + [("stack", 0, 1), ("init_v",), ("v", 0), ("init_stacks",)]
    for g in range(G + LAG + 3):
        for u in range(UNITS):
            n = g * UNITS + u
            if g < G:
                schedule.append(("pass1", n))
            if 0 <= g - LAG < G:
                schedule.append(("pass2", n - LAG * UNITS))
            if 0 <= n - LAG * UNITS - PV_LAG < G * UNITS:
                schedule.append(("pv", n - LAG * UNITS - PV_LAG))
            schedule += extra.pop((g, u), [])
    assert not extra
    ahead = {0: (0,), 1: (1,), 2: (2,), 3: (3, 4), 4: (5,), 5: (6, 7), 6: (8,), 7: (9,)}
    for i in range(B * E + 1):
        if i < B * E:
            schedule.append(("fc1", i))
        if i > 0:
            schedule.append(("fc2", i - 1))
            b, e = divmod(i - 1, E)
            if b + 1 < B:
                schedule += [(ROUTE[r], b + 1) for r in ahead[e]]
            if e == E - 1:
                schedule.append(("store", b))

    MISC = ("xnT", "q", "k", "v", "maxT", "oT", "onT", "proj", "hidden_bias",
            "xfT", "zT", "gate", "combT", "fc2_bias")
    misc_no = {}
    for s in schedule:
        if s[0] in MISC:
            misc_no[s] = len(misc_no)
    fills = [s for s in schedule if s[0] in ("pass1", "pass2")]
    slot_no = {s: i for i, s in enumerate(fills)}
    split_no = {}
    for s in schedule:
        if s[0] == "split":
            split_no[s] = len(split_no)

    with ExitStack() as ctx:
        def sb(name, shape, dt=F32):
            return ctx.enter_context(nc.sbuf_tensor(name, shape, dt))

        def sem(name):
            return ctx.enter_context(nc.semaphore(name))

        slots = ctx.enter_context(nc.psum_tensor("slots", [P, 2 * SLOTS, 512], F32))
        acc_bank = ctx.enter_context(nc.psum_tensor("acc_bank", [P, 512], F32))
        misc = ctx.enter_context(nc.psum_tensor("misc", [P, 512], F32))

        ident = sb("ident", [P, P])
        ident_b = sb("ident_b", [P, P], BF16)
        causal = sb("causal", [P, HPG, P], BF16)
        minus_half = sb("minus_half", [P, NT])
        expert_idi = sb("expert_idi", [P, NT, E], mybir.dt.int32)
        expert_ids = sb("expert_ids", [P, NT, E])
        wqkv_s = sb("wqkv_s", [P, 3, P])
        bqk_s = sb("bqk_s", [P, 2])
        bv_s = sb("bv_s", [P, P])
        wp_s = sb("wp_s", [P, P])
        bp_s = sb("bp_s", [P, P])
        wg_s = sb("wg_s", [P, E])
        alpha_s = sb("alpha_s", [P, E])
        lnw_s = sb("lnw_s", [P, E])
        lnb_s = sb("lnb_s", [P, E])
        b1_s = sb("b1_s", [P, E * NK])
        b2_s = sb("b2_s", [E, C])
        w1_s = sb("w1_s", [P, E, F])
        w2_s = sb("w2_s", [P, E * NK, C])
        xt = sb("xt", [P, B * NT, C])
        stats = sb("stats", [P, NT, 6])
        mean_var = sb("mean_var", [P, NT, 2])
        var_eps = sb("var_eps", [P, NT])
        rstd = sb("rstd", [P, NT])
        xn = sb("xn", [P, NT, C])
        xnT = sb("xnT", [P, T])
        qk32 = sb("qk32", [P, 2, T])
        rest = sb("rest", [P, 2, T])
        parts = sb("parts", [P, 2, PARTS, T], BF16)
        stack = [[sb(f"stack_{'qk'[i]}{j}", [P, H, T], BF16) for j in range(2)] for i in range(2)]
        v1 = sb("v1", [P, 2, NT, H, 32])
        row_max = sb("row_max", [P, 2, HPG, NT])
        mx32 = sb("mx32", [NT * HPG, 2, P])
        mx_rest = sb("mx_rest", [NT * HPG, P])
        mx_parts = sb("mx_parts", [NT * HPG, 2, PARTS, P], BF16)
        probs = sb("probs", [P, P_RING, 2 * 512])
        oT = sb("oT", [P, 2, T])
        inv_sum = sb("inv_sum", [P, NT, HPG])
        on = sb("on", [P, NT, C])
        onT = sb("onT", [P, T])
        xf = sb("xf", [P, NT, C])
        z = sb("z", [P, NT, C])
        xfT = sb("xfT", [P, T])
        zT = sb("zT", [P, 2, T])
        gate_in = sb("gate_in", [P, NT, E])
        top = sb("top", [P, NT, E])
        top_at = sb("top_at", [P, NT, E], U32)
        top_atf = sb("top_atf", [P, NT, 2])
        diff = sb("diff", [P, NT])
        second = sb("second", [P, NT])
        denom = sb("denom", [P, NT])
        gates = sb("gates", [P, NT, 2])
        pick = sb("pick", [P, 2, NT, E])
        comb = sb("comb", [P, 2, NT, E])
        combT = sb("combT", [E, T])
        hidden = probs[:, :, :].rearrange("p (i a) (c t) -> p i (a c) t", i=2, c=2)

        s_x = [sem(f"s_x{b}") for b in range(B)]
        s_wqkv, s_wp, s_w1, s_w2, s_small = (sem(n) for n in ("s_wqkv", "s_wp", "s_w1", "s_w2", "s_small"))
        s_pool = sem("s_pool")
        s_ident = sem("s_ident")
        s_vinit = sem("s_vinit")
        s_zero, s_zero1 = sem("s_zero"), sem("s_zero1")
        s_ln = sem("s_ln")
        s_var = sem("s_var")
        s_rstd = sem("s_rstd")
        s_xn, s_xf, s_z = sem("s_xn"), sem("s_xf"), sem("s_z")
        s_fill = sem("s_fill")
        s_free = sem("s_free")
        s_split = sem("s_split")
        s_stack = [[sem(f"s_stack_{'qk'[i]}{j}") for j in range(2)] for i in range(2)]
        s_pass1, s_max = sem("s_pass1"), sem("s_max")
        s_pass2, s_exp = sem("s_pass2"), sem("s_exp")
        s_cut, s_pv = sem("s_cut"), sem("s_pv")
        s_mpart = sem("s_mpart")
        s_mrow = [sem(f"s_mrow{j}") for j in range(2)]
        s_pvout = sem("s_pvout")
        s_inv = sem("s_inv")
        s_resid = sem("s_resid")
        s_w1s = sem("s_w1s")
        s_diff, s_second, s_comb = sem("s_diff"), sem("s_second"), sem("s_comb")
        s_h, s_gelu, s_y, s_acc = sem("s_h"), sem("s_gelu"), sem("s_y"), sem("s_acc")
        s_out = sem("s_out")

        def wait(eng, semaphore, value):
            if value > 0:
                eng.wait_ge(semaphore, value)

        def unit_of(n):
            g, u = divmod(n, UNITS)
            blocks, heads = UNIT[u]
            return g, u, blocks * P, heads

        def columns(n, slot):
            _, u, w, heads = unit_of(n)
            two = slots[:, 2 * slot:2 * slot + 2, :]
            if w > 256:
                return two[:, :, 0:w]
            if w == 256:
                return two.rearrange("p k (a w) -> p (k a) w", w=w)
            return slots[:, 2 * slot, :].rearrange("p (a w) -> p a w", w=w)

        def probs_of(n):
            _, _, w, heads = unit_of(n)
            return probs[:, n % P_RING, 0:len(heads) * w].rearrange("p (h w) -> p h w", w=w)

        def wait_slot(eng, stage):
            i = slot_no[stage]
            if i >= SLOTS:
                kind, n = fills[i - SLOTS]
                wait(eng, s_max if kind == "pass1" else s_exp, n + 1)
            return i % SLOTS

        def wait_filled(eng, stage):
            wait(eng, s_fill, misc_no[stage] + 1)

        block = ctx.enter_context(nc.Block())

        def walk(handlers):
            for s in schedule:
                if s[0] in handlers:
                    handlers[s[0]](*s[1:])

        @block.sync
        def _(sp):
            def load_x(b):
                sp.dma_start(xt[:, NT * b:NT * b + NT, :],
                             x[b].rearrange("(n p) c -> p n c", p=P)).then_inc(s_x[b], 16)

            load_x(0)
            for i, w in enumerate((wqT, wkT, wvT)):
                sp.dma_start(wqkv_s[:, i, :], w).then_inc(s_wqkv, 16)
            for i, v in enumerate((bq, bk)):
                sp.dma_start(bqk_s[:, i:i + 1], v.rearrange("(p a) -> p a", a=1)).then_inc(s_wqkv, 16)
            sp.dma_start(bv_s[:, :], bv.rearrange("(a c) -> a c", a=1).broadcast_to([P, C])).then_inc(s_wqkv, 16)
            load_x(1)
            sp.dma_start(wp_s[:, :], wpT).then_inc(s_wp, 16)
            sp.dma_start(bp_s[:, :], bp.rearrange("(a c) -> a c", a=1).broadcast_to([P, C])).then_inc(s_wp, 16)
            sp.dma_start(w1_s[:, :, :], w1.rearrange("e h f -> h e f")).then_inc(s_w1, 16)
            sp.dma_start(lnw_s[:, :], lnwT).then_inc(s_small, 16)
            sp.dma_start(lnb_s[:, :], lnbT).then_inc(s_small, 16)
            sp.dma_start(b1_s[:, :], b1T).then_inc(s_small, 16)
            sp.dma_start(wg_s[:, :], wg).then_inc(s_small, 16)
            sp.dma_start(b2_s[:, :], b2).then_inc(s_small, 16)
            sp.dma_start(alpha_s[:, :], alpha.rearrange("(a c) -> a c", a=1).broadcast_to([P, E])).then_inc(s_small, 16)

            def stack_up(b, i):
                wait(sp, s_split, split_no[("split", b, i, 3)] + 1)
                wait(sp, (s_zero, s_zero1)[b % 2], 1)
                wait(sp, s_pass2, (b - 1) * NG * UNITS)
                for first, count, part, step in (Q_PRODUCTS, K_PRODUCTS)[i]:
                    for j in range(count):
                        r = (first + j) * D
                        sp.dma_start(stack[i][b % 2][r:r + D, :, :], parts[:, i, part + j * step, :])\
                          .then_inc(s_stack[i][b % 2], 16)
                if i == 1 and b == 0:
                    sp.dma_start(w2_s[:, :, :], w2.rearrange("e (k p) h -> p (e k) h", p=P)).then_inc(s_w2, 16)
                    for later in range(2, B):
                        load_x(later)

            def max_rows(g):
                b, hg = divmod(g, NG)
                wait(sp, s_mpart, 4 * (g + 1))
                for part in range(PARTS):
                    dst = stack[0][b % 2][MAX_ROW + part:MAX_ROW + part + 1, HPG * hg:HPG * hg + HPG, :]
                    sp.dma_start(dst, mx_parts[:, g % 2, part, :]).then_inc(s_mrow[g % 2], 16)

            def store(b):
                wait(sp, s_acc, E * (b + 1))
                sp.dma_start(out[b].rearrange("(n p) c -> p n c", p=P),
                             xt[:, NT * b:NT * b + NT, :]).then_inc(s_out, 16)

            walk({"stack": stack_up, "max_parts": max_rows, "store": store})
            sp.wait_ge(s_out, 16 * B)

        @block.tensor
        def _(pe):
            def claim(stage):
                wait(pe, s_free, misc_no[stage])

            def transpose_tiles(stage, src):
                for n in range(NT):
                    mm = pe.transpose(misc[:, n * P:n * P + P], src[:, n, :], ident[:, :])
                mm.then_inc(s_fill, 1)

            def turn_xn(b):
                claim(("xnT", b))
                if b == 0:
                    pe.wait_ge(s_ident, 1)
                wait(pe, s_xn, b + 1)
                transpose_tiles(("xnT", b), xn)

            def project(b, i, name):
                claim((name, b))
                pe.wait_ge(s_wqkv, 16 * 6)
                pe.matmul(misc[:, :], wqkv_s[:, i, :], xnT[:, :], start=True, stop=True).then_inc(s_fill, 1)

            def project_v(b):
                claim(("v", b))
                for n in range(NT):
                    mm = pe.matmul(misc[:, n * P:n * P + P], xnT[:, n * P:n * P + P], wqkv_s[:, 2, :],
                                   start=True, stop=True)
                mm.then_inc(s_fill, 1)

            def pass1(n):
                g, u, w, heads = unit_of(n)
                b, hg = divmod(g, NG)
                slot = wait_slot(pe, ("pass1", n))
                if n % (NG * UNITS) == 0:
                    for i in range(2):
                        pe.wait_ge(s_stack[i][b % 2], 16 * 6 * (b // 2 + 1))
                cols = columns(n, slot)
                blk = w // P - 1
                q, k = stack[0][b % 2], stack[1][b % 2]
                banks = 1 if w == P else 2
                per_bank = len(heads) // banks
                for i in range(banks):
                    pe.matmul(cols[:, per_bank * i:per_bank * i + per_bank, w - P:w], ident_b[:, :],
                              causal[:, 0:per_bank, :], start=True, stop=False, skip_group_check=True)
                for i, h in enumerate(heads):
                    hh = HPG * hg + h
                    mm = pe.matmul(cols[:, i, :], q[0:K1, hh, blk * P:blk * P + P], k[0:K1, hh, 0:w],
                                   start=False, stop=True, skip_group_check=True)
                mm.then_inc(s_pass1, 1)

            def pass2(n):
                g, u, w, heads = unit_of(n)
                b, hg = divmod(g, NG)
                slot = wait_slot(pe, ("pass2", n))
                if u == 0:
                    pe.wait_ge(s_mrow[g % 2], 16 * PARTS * (g // 2 + 1))
                cols = columns(n, slot)
                blk = NT - w // P
                q, k = stack[0][b % 2], stack[1][b % 2]
                for i, h in enumerate(heads):
                    hh = HPG * hg + h
                    mm = pe.matmul(cols[:, i, :], k[0:K2, hh, blk * P:blk * P + P], q[0:K2, hh, blk * P:T],
                                   start=True, stop=True)
                mm.then_inc(s_pass2, 1)

            def pv(n):
                g, u, w, heads = unit_of(n)
                b, hg = divmod(g, NG)
                blk = NT - w // P
                wait(pe, s_cut, n + 1)
                if u == 0:
                    wait(pe, s_pvout, g)
                    wait(pe, s_free, misc_no[("v", b)] + 1)
                p = probs_of(n)
                for i, h in enumerate(heads):
                    mm = pe.matmul(acc_bank[32 * h:32 * h + 32, blk * P:T], v1[:, b % 2, blk, HPG * hg + h, :],
                                   p[:, i, :], start=(blk == 0), stop=(blk == NT - 1),
                                   tile_position=(0, 32 * h))
                mm.then_inc(s_pv, 1)

            def turn_max(g):
                claim(("maxT", g))
                wait(pe, s_max, UNITS * (g + 1))
                pe.transpose(misc[0:NT * HPG, 0:P], row_max[:, g % 2, :, :].rearrange("p h n -> p (h n)"), ident[:, :]).then_inc(s_fill, 1)

            def turn_o(g):
                claim(("oT", g))
                wait(pe, s_pvout, g + 1)
                for n in range(NT):
                    mm = pe.transpose(misc[:, n * P:n * P + P], oT[:, g % 2, n * P:n * P + P], ident[:, :])
                mm.then_inc(s_fill, 1)

            def turn_on(b):
                claim(("onT", b))
                transpose_tiles(("onT", b), on)

            def project_out(b):
                claim(("proj", b))
                pe.wait_ge(s_wp, 32)
                for n in range(NT):
                    mm = pe.matmul(misc[:, n * P:n * P + P], onT[:, n * P:n * P + P], wp_s[:, :],
                                   start=True, stop=True)
                mm.then_inc(s_fill, 1)

            def hidden_bias():
                claim(("hidden_bias",))
                pe.wait_ge(s_w1, 16)
                pe.wait_ge(s_small, 16 * 6)
                for e in range(E):
                    for k in range(NK):
                        i = e * NK + k
                        mm = pe.matmul(misc[:, i:i + 1], w1_s[:, e, k * P:k * P + P], lnb_s[:, e:e + 1],
                                       start=True, stop=True)
                mm.then_inc(s_fill, 1)

            def turn_xf(b):
                claim(("xfT", b))
                wait(pe, s_xf, b + 1)
                transpose_tiles(("xfT", b), xf)

            def turn_z(b):
                claim(("zT", b))
                wait(pe, s_z, b + 1)
                transpose_tiles(("zT", b), z)

            def gate(b):
                claim(("gate", b))
                for n in range(NT):
                    mm = pe.matmul(misc[:, n * E:n * E + E], xfT[:, n * P:n * P + P], wg_s[:, :],
                                   start=True, stop=True)
                mm.then_inc(s_fill, 1)

            def turn_comb(b):
                claim(("combT", b))
                wait(pe, s_comb, b + 1)
                for n in range(NT):
                    mm = pe.transpose(misc[0:E, n * P:n * P + P], comb[:, b % 2, n, :], ident[:, :])
                mm.then_inc(s_fill, 1)

            def fc2_bias(b):
                claim(("fc2_bias", b))
                for n in range(NT):
                    mm = pe.matmul(misc[:, n * P:n * P + P], combT[:, n * P:n * P + P], b2_s[:, :],
                                   start=True, stop=True)
                mm.then_inc(s_fill, 1)

            def fc1(i):
                b, e = divmod(i, E)
                if i == 0:
                    wait(pe, s_exp, G * UNITS)
                    wait(pe, s_w1s, E)
                if e == 0:
                    wait(pe, s_free, misc_no[("zT", b)] + 1)
                for k in range(NK):
                    j = i * NK + k
                    wait(pe, s_gelu, j + 1 - 2 * SLOTS)
                    pe.matmul(slots[:, j % (2 * SLOTS), :], w1_s[:, e, k * P:k * P + P], zT[:, b % 2, :],
                              start=True, stop=True).then_inc(s_h, 1)

            def fc2(i):
                e = i % E
                if i == 0:
                    pe.wait_ge(s_w2, 16)
                    wait(pe, s_pvout, G)
                wait(pe, s_gelu, NK * (i + 1))
                wait(pe, s_acc, i)
                for n in range(NT):
                    for k in range(NK):
                        mm = pe.matmul(acc_bank[:, n * P:n * P + P], hidden[:, i % 2, k, n * P:n * P + P],
                                       w2_s[:, e * NK + k, :], start=(k == 0), stop=(k == NK - 1))
                mm.then_inc(s_y, 1)

            walk({"xnT": turn_xn, "q": lambda b: project(b, 0, "q"), "k": lambda b: project(b, 1, "k"),
                  "v": project_v, "pass1": pass1, "pass2": pass2, "pv": pv, "maxT": turn_max, "oT": turn_o,
                  "onT": turn_on, "proj": project_out, "hidden_bias": hidden_bias, "xfT": turn_xf,
                  "zT": turn_z, "gate": gate, "combT": turn_comb, "fc2_bias": fc2_bias, "fc1": fc1, "fc2": fc2})

        @block.scalar
        def _(act):
            def copy_misc(stage, dst):
                wait_filled(act, stage)
                act.activation(dst, misc[:, :], ACT.Copy).then_inc(s_free, 1)

            def turn_xn(b):
                copy_misc(("xnT", b), xnT[:, :])

            def biased(b, i, name):
                wait_filled(act, (name, b))
                if b > 0:
                    wait(act, s_split, split_no[("split", b - 1, i, 3)] + 1)
                act.activation(qk32[:, i, :], misc[:, :], ACT.Identity, bias=bqk_s[:, i:i + 1]).then_inc(s_free, 1)

            def pass2(n):
                slot = slot_no[("pass2", n)] % SLOTS
                wait(act, s_pass2, n + 1)
                wait(act, s_pv, n + 1 - P_RING)
                act.activation(probs_of(n), columns(n, slot), ACT.Exp, scale=SCALE).then_inc(s_exp, 1)

            def pv_out(g):
                wait(act, s_pv, UNITS * (g + 1))
                if g >= 2:
                    wait(act, s_fill, misc_no[("oT", g - 2)] + 1)
                act.activation(oT[:, g % 2, :], acc_bank[:, :], ACT.Copy).then_inc(s_pvout, 1)

            def second_gate(b):
                wait(act, s_diff, b + 1)
                act.activation(second[:, :], diff[:, :], ACT.Exp).then_inc(s_second, 1)

            def fc1(i):
                b, e = divmod(i, E)
                if i == 0:
                    wait(act, s_pv, G * UNITS)
                wait(act, s_y, i - 1)
                for k in range(NK):
                    j = i * NK + k
                    wait(act, s_h, j + 1)
                    act.activation(hidden[:, i % 2, k, :], slots[:, j % (2 * SLOTS), :], ACT.Gelu_apprx_tanh,
                                   bias=b1_s[:, e * NK + k:e * NK + k + 1]).then_inc(s_gelu, 1)

            def turn_comb(b):
                wait_filled(act, ("combT", b))
                act.activation(combT[:, :], misc[0:E, :], ACT.Copy).then_inc(s_free, 1)

            walk({"xnT": turn_xn, "q": lambda b: biased(b, 0, "q"), "k": lambda b: biased(b, 1, "k"),
                  "pass2": pass2, "pv_out": pv_out, "onT": lambda b: copy_misc(("onT", b), onT[:, :]),
                  "xfT": lambda b: copy_misc(("xfT", b), xfT[:, :]),
                  "zT": lambda b: copy_misc(("zT", b), zT[:, b % 2, :]),
                  "r_top": second_gate, "combT": turn_comb, "fc1": fc1})

        @block.vector
        def _(dve):
            chain = [0]

            def link(ins):
                ins.then_inc(s_ln, 1)
                chain[0] += 1
                dve.wait_ge(s_ln, chain[0])

            minus_ones = float(np.array([0xBF80BF80], np.uint32).view(np.float32)[0])
            for i in range(2):
                dve.memset(stack[i][0][0:MAX_ROW, :, :].bitcast(F32), 0.0)
            dve.memset(stack[1][0][MAX_ROW:K2, :, :].bitcast(F32), minus_ones).then_inc(s_zero, 1)
            variance_no = [0]

            def variance(src):
                for n in range(NT):
                    last = dve.bn_stats(stats[:, n, :], src[:, n, :])
                link(last)
                for n in range(NT):
                    last = dve.bn_aggr(mean_var[:, n, :], stats[:, n, :])
                link(last)
                dve.tensor_scalar(var_eps[:, :], mean_var[:, :, 1], EPS, None, ALU.add).then_inc(s_var, 1)
                variance_no[0] += 1

            def normalise(dst, src):
                wait(dve, s_rstd, variance_no[0])
                for n in range(NT):
                    last = dve.tensor_scalar(dst[:, n, :], src[:, n, :], mean_var[:, n, 0:1], rstd[:, n:n + 1],
                                             ALU.subtract, ALU.mult)
                return last

            def ln_stats(b):
                dve.wait_ge(s_x[b], 16)
                variance(xt[:, NT * b:NT * b + NT, :])

            def ln_apply(b):
                if b > 0:
                    wait_filled(dve, ("xnT", b - 1))
                normalise(xn, xt[:, NT * b:NT * b + NT, :]).then_inc(s_xn, 1)

            def put_v(b):
                wait_filled(dve, ("v", b))
                if b == 0:
                    dve.wait_ge(s_vinit, 1)
                wait(dve, s_pv, (b - 1) * NG * UNITS)
                dve.tensor_tensor(v1[:, b % 2, :, :, 0:D],
                                  misc[:, :].rearrange("p (n h d) -> p n h d", h=H, d=D),
                                  bv_s[:, :].rearrange("p (a h d) -> p a h d", a=1, h=H)
                                  .broadcast_to([P, NT, H, D]), ALU.add).then_inc(s_free, 1)

            def pass1(n):
                g, u, w, heads = unit_of(n)
                slot = slot_no[("pass1", n)] % SLOTS
                wait(dve, s_pass1, n + 1)
                dve.tensor_reduce(row_max[:, g % 2, heads[0]:heads[-1] + 1, w // P - 1], columns(n, slot), AX.X, ALU.max)\
                   .then_inc(s_max, 1)

            def turn_max(g):
                wait_filled(dve, ("maxT", g))
                if g >= 2:
                    wait(dve, s_mpart, 4 * (g - 1))
                dve.tensor_copy(mx32[:, g % 2, :], misc[0:NT * HPG, 0:P]).then_inc(s_free, 1)

            def turn_o(g):
                b, hg = divmod(g, NG)
                wait_filled(dve, ("oT", g))
                o = misc[:, :].rearrange("p (n h d) -> p n h d", h=HPG, d=32)
                dve.reciprocal(inv_sum[:, :, :], o[:, :, :, D]).then_inc(s_inv, 1)
                dve.wait_ge(s_inv, g + 1)
                if hg == 0 and b > 0:
                    wait_filled(dve, ("onT", b - 1))
                dst = on[:, :, HPG * D * hg:HPG * D * (hg + 1)].rearrange("p n (h d) -> p n h d", d=D)
                scale = inv_sum[:, :, :].rearrange("p n (h a) -> p n h a", a=1).broadcast_to([P, NT, HPG, D])
                dve.tensor_tensor(dst, o[:, :, :, 0:D], scale, ALU.mult).then_inc(s_free, 1)

            def project_out(b):
                wait_filled(dve, ("proj", b))
                wait(dve, s_resid, b + 1)
                tile = xt[:, NT * b:NT * b + NT, :]
                dve.tensor_tensor(tile, misc[:, :].rearrange("p (n c) -> p n c", c=C), tile, ALU.add)\
                   .then_inc(s_free, 1)

            def hidden_bias():
                wait_filled(dve, ("hidden_bias",))
                dve.tensor_tensor(b1_s[:, :], misc[:, 0:E * NK], b1_s[:, :], ALU.add).then_inc(s_free, 1)

            def stats1(b):
                wait(dve, s_free, misc_no[("proj", b)] + 1)
                variance(xt[:, NT * b:NT * b + NT, :])

            def make_xf(b):
                if b > 0:
                    wait_filled(dve, ("xfT", b - 1))
                normalise(xf, xt[:, NT * b:NT * b + NT, :]).then_inc(s_xf, 1)
                dve.wait_ge(s_xf, b + 1)
                variance(xf)

            def make_z(b):
                if b > 0:
                    wait_filled(dve, ("zT", b - 1))
                normalise(z, xf).then_inc(s_z, 1)

            def gate(b):
                wait_filled(dve, ("gate", b))
                dve.tensor_copy(gate_in[:, :, :], misc[:, 0:NT * E].rearrange("p (n e) -> p n e", e=E))\
                   .then_inc(s_free, 1)

            def top_two(b):
                wait(dve, s_free, misc_no[("gate", b)] + 1)
                for n in range(NT):
                    last = dve.max(top[:, n, :], gate_in[:, n, :])
                link(last)
                for n in range(NT):
                    last = dve.max_index(top_at[:, n, :], top[:, n, :], gate_in[:, n, :])
                link(last)
                wait(dve, s_second, b)
                dve.tensor_tensor(diff[:, :], top[:, :, 1], top[:, :, 0], ALU.subtract).then_inc(s_diff, 1)
                link(dve.tensor_copy(top_atf[:, :, :], top_at[:, :, 0:2]))
                for j in range(2):
                    last = dve.tensor_tensor(pick[:, j, :, :], expert_ids[:, :, :],
                                             top_atf[:, :, j:j + 1].broadcast_to([P, NT, E]), ALU.is_equal)
                link(last)

            def combine(b):
                wait(dve, s_second, b + 1)
                link(dve.tensor_scalar(denom[:, :], second[:, :], 1.0, None, ALU.add))
                link(dve.reciprocal(gates[:, :, 0], denom[:, :]))
                link(dve.tensor_tensor(gates[:, :, 1], gates[:, :, 0], second[:, :], ALU.mult))
                for j in range(2):
                    last = dve.tensor_tensor(pick[:, j, :, :], pick[:, j, :, :],
                                             gates[:, :, j:j + 1].broadcast_to([P, NT, E]), ALU.mult)
                link(last)
                link(dve.tensor_tensor(pick[:, 0, :, :], pick[:, 0, :, :], pick[:, 1, :, :], ALU.add))
                dve.tensor_tensor(comb[:, b % 2, :, :], pick[:, 0, :, :],
                                  alpha_s[:, :].rearrange("p (a e) -> p a e", a=1).broadcast_to([P, NT, E]),
                                  ALU.mult).then_inc(s_comb, 1)

            def fc2_bias(b):
                wait_filled(dve, ("fc2_bias", b))
                tile = xt[:, NT * b:NT * b + NT, :]
                dve.tensor_tensor(tile, misc[:, :].rearrange("p (n c) -> p n c", c=C), tile, ALU.add)\
                   .then_inc(s_free, 1)

            def fc2(i):
                b, e = divmod(i, E)
                wait(dve, s_y, i + 1)
                if e == 0:
                    wait(dve, s_free, misc_no[("fc2_bias", b)] + 1)
                    wait(dve, s_comb, b + 1)
                wait(dve, s_acc, i)
                for n in range(NT):
                    tile = xt[:, NT * b + n, :]
                    last = dve.scalar_tensor_tensor(tile, acc_bank[:, n * P:n * P + P], comb[:, b % 2, n, e:e + 1],
                                                    tile, ALU.mult, ALU.add)
                last.then_inc(s_acc, 1)

            walk({"ln_stats": ln_stats, "ln_apply": ln_apply, "v": put_v, "pass1": pass1, "maxT": turn_max,
                  "oT": turn_o, "proj": project_out, "hidden_bias": hidden_bias, "r_stats1": stats1,
                  "r_xf": make_xf, "r_z": make_z, "gate": gate, "r_top": top_two, "r_comb": combine,
                  "fc2_bias": fc2_bias, "fc2": fc2})

        @block.gpsimd
        def _(pool):
            steps = [0]

            def link(ins):
                ins.then_inc(s_pool, 1)
                steps[0] += 1
                pool.wait_ge(s_pool, steps[0])

            link(pool.memset(minus_half[:, :], -0.5))
            link(pool.memset(ident[:, :], 0.0))
            link(pool.affine_select(out=ident[:, :], in_=ident[:, :], compare_op=ALU.not_equal, fill=1.0,
                                    base=0, pattern=[[-1, P]], channel_multiplier=1))
            link(pool.tensor_copy(ident_b[:, :], ident[:, :]))
            link(pool.memset(causal[:, :, :], 0.0))
            pool.affine_select(out=causal[:, :, :], in_=causal[:, :, :], compare_op=ALU.is_ge, fill=NEG,
                               base=0, pattern=[[0, HPG], [-1, P]], channel_multiplier=1).then_inc(s_ident, 1)
            variance_no = [0]

            def rsqrt(*_):
                variance_no[0] += 1
                wait(pool, s_var, variance_no[0])
                pool.tensor_tensor(rstd[:, :], var_eps[:, :], minus_half[:, :], ALU.pow).then_inc(s_rstd, 1)

            def init_v(*_):
                link(pool.memset(v1[:, :, :, :, :].rearrange("p i n h d -> p (i n h) d"), 0.0))
                pool.memset(v1[:, :, :, :, D:D + 1].rearrange("p i n h d -> p (i n h) d"), 1.0).then_inc(s_vinit, 1)
                pool.wait_ge(s_vinit, 1)

            def init_stacks(*_):
                minus_ones = float(np.array([0xBF80BF80], np.uint32).view(np.float32)[0])
                for i in range(2):
                    link(pool.memset(stack[i][1][0:MAX_ROW, :, :].bitcast(F32), 0.0))
                pool.memset(stack[1][1][MAX_ROW:K2, :, :].bitcast(F32), minus_ones).then_inc(s_zero1, 1)
                pool.wait_ge(s_zero1, 1)
                link(pool.iota(expert_idi[:, :, :], pattern=[[0, NT], [1, E]], base=0, channel_multiplier=0))
                link(pool.tensor_copy(expert_ids[:, :, :], expert_idi[:, :, :]))

            def split(b, i, step):
                source, part = qk32[:, i, :], parts[:, i, :, :]
                if step == 0:
                    wait_filled(pool, (("q", b), ("k", b))[i])
                    wait(pool, s_free, misc_no[(("q", b), ("k", b))[i]] + 1)
                    if b > 0:
                        pool.wait_ge(s_stack[i][(b - 1) % 2], 16 * 6 * ((b - 1) // 2 + 1))
                if split_no[("split", b, i, step)] > 0:
                    wait(pool, s_split, split_no[("split", b, i, step)])
                if step == 0:
                    ins = pool.tensor_copy(part[:, 0, :], source)
                elif step == 1:
                    ins = pool.tensor_tensor(rest[:, i, :], source, part[:, 0, :], ALU.subtract)
                elif step == 2:
                    ins = pool.tensor_copy(part[:, 1, :], rest[:, i, :])
                else:
                    ins = pool.tensor_tensor(part[:, 2, :], rest[:, i, :], part[:, 1, :], ALU.subtract)
                ins.then_inc(s_split, 1)

            def pass2(n):
                g, u, w, heads = unit_of(n)
                wait(pool, s_exp, n + 1)
                diag = probs_of(n)[:, :, 0:P]
                pool.affine_select(out=diag, in_=diag, compare_op=ALU.is_ge, fill=0.0, base=0,
                                   pattern=[[0, len(heads)], [1, P]], channel_multiplier=-1).then_inc(s_cut, 1)

            def max_parts(g):
                j = g % 2
                wait(pool, s_free, misc_no[("maxT", g)] + 1)
                if g >= 2:
                    pool.wait_ge(s_mrow[j], 16 * PARTS * (g // 2))
                source, part = mx32[:, j, :], mx_parts[:, j, :, :]
                for step in range(4):
                    if step == 0:
                        ins = pool.tensor_copy(part[:, 0, :], source)
                    elif step == 1:
                        ins = pool.tensor_tensor(mx_rest[:, :], source, part[:, 0, :], ALU.subtract)
                    elif step == 2:
                        ins = pool.tensor_copy(part[:, 1, :], mx_rest[:, :])
                    else:
                        ins = pool.tensor_tensor(part[:, 2, :], mx_rest[:, :], part[:, 1, :], ALU.subtract)
                    ins.then_inc(s_mpart, 1)
                    pool.wait_ge(s_mpart, 4 * g + step + 1)

            def residual(b):
                wait(pool, s_xn, b + 1)
                pool.wait_ge(s_wp, 32)
                tile = xt[:, NT * b:NT * b + NT, :]
                pool.tensor_tensor(tile, tile, bp_s[:, :].rearrange("p (a c) -> p a c", a=1)
                                   .broadcast_to([P, NT, C]), ALU.add).then_inc(s_resid, 1)

            def scale_w1(e):
                wait(pool, s_free, misc_no[("hidden_bias",)] + 1)
                pool.tensor_scalar(w1_s[:, e, :], w1_s[:, e, :], lnw_s[:, e:e + 1], None, ALU.mult)\
                    .then_inc(s_w1s, 1)

            walk({"ln_stats": rsqrt, "r_stats1": rsqrt, "r_xf": rsqrt, "init_v": init_v,
                  "init_stacks": init_stacks, "split": split, "pass2": pass2, "max_parts": max_parts,
                  "residual": residual, "scale_w1": scale_w1})


NAMES = ("x", "wqT", "wkT", "wvT", "bq", "bk", "bv", "wpT", "bp", "wg", "alpha", "lnwT", "lnbT",
         "w1", "b1T", "w2", "b2")


def kernel(L0_attn_x, L0_attn_W_qkv, L0_attn_b_qkv, L0_attn_W_proj, L0_attn_b_proj, L0_ffn_Wg, L0_ffn_alpha,
           L0_ffn_ln_w, L0_ffn_ln_b, L0_ffn_fc1_w, L0_ffn_fc1_b, L0_ffn_fc2_w, L0_ffn_fc2_b):
    import numpy as _np
    import concourse.bacc as _bacc
    from concourse import mybir as _mybir
    from concourse.bass_utils import run_bass_kernel_spmd as _run

    w_qkv, b_qkv = _np.asarray(L0_attn_W_qkv), _np.asarray(L0_attn_b_qkv)
    C = w_qkv.shape[1]
    E, F = _np.shape(L0_ffn_fc1_b)
    b1 = _np.asarray(L0_ffn_fc1_b).reshape(E, F // C, C).transpose(2, 0, 1).reshape(C, E * (F // C))
    wq, wk = (w_qkv[i * C:i * C + C].reshape(16, C // 16, C).transpose(1, 0, 2).reshape(C, C) for i in range(2))
    bq, bk = (b_qkv[i * C:i * C + C].reshape(16, C // 16).T.reshape(C) for i in range(2))
    values = (
        L0_attn_x, wq.T, wk.T, w_qkv[2 * C:3 * C].T, bq, bk, b_qkv[2 * C:3 * C],
        _np.asarray(L0_attn_W_proj).T, L0_attn_b_proj, L0_ffn_Wg, L0_ffn_alpha,
        _np.asarray(L0_ffn_ln_w).T, _np.asarray(L0_ffn_ln_b).T, L0_ffn_fc1_w, b1, L0_ffn_fc2_w, L0_ffn_fc2_b,
    )
    nc = _bacc.Bacc("TRN2", target_bir_lowering=False, num_devices=1)
    arrays, args = {}, []
    for name, value in zip(NAMES, values):
        a = _np.ascontiguousarray(value)
        arrays[f"in_{name}"] = a
        args.append(nc.dram_tensor(f"in_{name}", a.shape, _mybir.dt.from_np(a.dtype), kind="ExternalInput").ap())
    out = nc.dram_tensor("out", arrays["in_x"].shape, _mybir.dt.float32, kind="ExternalOutput").ap()
    build(nc, *args, out)
    r = _run(nc, [arrays], core_ids=[0])
    return r.results[0]["out"]
```

```python
import math
from contextlib import ExitStack

import numpy as np

import concourse.bass as bass
from concourse import mybir

F32, F32R, BF16, U32 = mybir.dt.float32, mybir.dt.float32r, mybir.dt.bfloat16, mybir.dt.uint32
ALU = mybir.AluOpType
ACT = mybir.ActivationFunctionType
AX = mybir.AxisListType

P = 128
EPS = 1e-5
NEG = -3.0e38
PARTS = 3
Q_PRODUCTS = ((0, 3, 0, 0), (3, 2, 1, 0), (5, 1, 2, 0))
K_PRODUCTS = ((0, 3, 0, 1), (3, 2, 0, 1), (5, 1, 0, 1))
MAX_ROW = 96
K1, K2 = MAX_ROW, MAX_ROW + PARTS
HPG = 4
UNIT = tuple((blocks, tuple(range(h, h + n))) for blocks, n in ((4, 1), (3, 1), (2, 2), (1, 4))
             for h in range(0, HPG, n))
UNITS = len(UNIT)
ROW_END = tuple(max(u for u in range(UNITS) if UNIT[u][0] == blocks) for blocks in (4, 3, 2, 1))
LAG = 2
PV_LAG = 5
SLOTS = 6
P_RING = 12
FC1_SLOTS = SLOTS - 1
POOL_CHUNK = 2
H_RING = 4
GATE_RING = 4


def build(nc, x, wqT, wkT, wvT, bq, bk, bv, wpT, bp, wg, alpha, lnwT, lnbT, w1, b1T, w2, b2, out):
    B, T, C = x.shape
    E, F = w1.shape[0], w1.shape[2]
    D = 8
    H = C // D
    NT = T // P
    NG = H // HPG
    G = B * NG
    NK = F // P
    SCALE = float(D) ** -0.5

    extra = {}

    def at(g, u, *stage):
        extra.setdefault((g, u), []).append(stage)

    for b in range(1, B):
        g = NG * (b - 1)
        at(g, 0, "ln_stats", b)
        at(g, 1, "ln_agg", b)
        at(g, 3, "ln_apply", b)
        at(g + 1, 0, "xnT", b)
        at(g + 1, 3, "q", b)
        for i in range(4):
            at(g + 1, 5 + i, "split", b, 0, i)
        at(g + 1, 10, "stack", b, 0)
        at(g + 2, 0, "k", b)
        for i in range(4):
            at(g + 2, 2 + i, "split", b, 1, i)
        at(g + 2, 7, "stack", b, 1)
        at(g + 3, 0, "v", b)
    for g in range(G):
        at(g + 1, 0, "max_parts", g)
        at(g + 1, 6, "maxT", g)
        at(g + LAG + 1, PV_LAG, "pv_out", g)
        at(g + LAG + 1, 9, "oT", g)
        if g % NG == NG - 1:
            b = g // NG
            at(g + LAG, 0, "residual", b)
            at(g + LAG + 2, 3, "onT", b)
            at(g + LAG + 3, 0, "proj", b)
    for i in range(E // 2):
        at(4 * (i + 1) - 2 * (i % 2), 3, "hidden_bias", i)
    for e in range(E):
        at(18 + e, 7, "scale_w1", e)
    ROUTE = (("r_stats1", 9, 7), ("r_agg1", 9, 9), ("r_xf", 10, 4), ("r_stats2", 10, 7), ("r_agg2", 10, 9),
             ("r_z", 11, 4), ("xfT", 14, 3), ("zT", 18, 3),
             ("gate", 20, 3), ("r_top", 20, 6), ("r_exp", 20, 8), ("r_comb", 21, 4), ("combT", 22, 3), ("fc2_bias", 24, 3))
    for name, g, u in ROUTE:
        at(g, u, name, 0)

    MISC = ("xnT", "q", "k", "v", "maxT", "oT", "onT", "proj", "hidden_bias",
            "xfT", "zT", "gate", "combT", "fc2_bias", "outT")
    schedule, unread = [], []

    def read_misc():
        while unread:
            schedule.append(("read", unread.pop()))

    def add(*stages):
        for s in stages:
            if s[0] in MISC:
                read_misc()
                unread.append(s)
            schedule.append(s)

    add(("ln_stats", 0), ("ln_agg", 0), ("ln_apply", 0), ("xnT", 0), ("q", 0), ("k", 0))
    read_misc()
    for step in range(4):
        add(("split", 0, 0, step), ("split", 0, 1, step))
    add(("stack", 0, 0), ("stack", 0, 1), ("init_v",), ("v", 0), ("init_stacks",))
    for g in range(G + LAG + 3):
        for u in range(UNITS):
            n = g * UNITS + u
            read_misc()
            if g < G:
                add(("pass1", n))
            if 0 <= g - LAG < G:
                add(("pass2", n - LAG * UNITS))
            pg, pu = divmod(n - LAG * UNITS - PV_LAG, UNITS)
            if 0 <= pg < G and pu in ROW_END:
                add(("pv", pg, ROW_END.index(pu)))
            add(*extra.pop((g, u), []))
    assert not extra
    AHEAD = {(0, 0): ("r_stats1", "r_agg1"), (1, 0): ("r_xf",), (1, 1): ("r_stats2", "r_agg2"),
             (2, 0): ("xfT",), (2, 1): ("r_z",), (3, 0): ("gate",), (3, 1): ("r_top",), (4, 0): ("zT",),
             (4, 1): ("r_exp",), (5, 0): ("r_comb",), (6, 0): ("combT",), (7, 0): ("fc2_bias",)}
    add(("split_w", 0), ("split_w", 1))
    for i in range(B * E + 2):
        if i < B * E:
            add(("fc1", i))
            if i + 2 < E:
                add(("split_w", i + 2))
        b, e = divmod(i - 1, E)
        for place in range(2):
            read_misc()
            if 0 <= b and b + 1 < B:
                add(*((r, b + 1) for r in AHEAD.get((e, place), ())))
            if place == 0:
                if i < B * E:
                    add(("gates", i))
                if 0 < i <= B * E:
                    add(("fc2", i - 1))
        if e == 0 and b > 0:
            add(("outT", b - 1))
    read_misc()

    misc_no = {}
    for s in schedule:
        if s[0] in MISC:
            misc_no[s] = len(misc_no)
    fills = [s for s in schedule if s[0] in ("pass1", "pass2")]
    slot_no = {s: i for i, s in enumerate(fills)}
    split_no = {}
    for s in schedule:
        if s[0] == "split":
            split_no[s] = len(split_no)

    with ExitStack() as ctx:
        def sb(name, shape, dt=F32, life=ctx):
            return life.enter_context(nc.sbuf_tensor(name, shape, dt))

        def sem(name):
            return ctx.enter_context(nc.semaphore(name))

        slots = ctx.enter_context(nc.psum_tensor("slots", [P, SLOTS, 512], F32))
        acc_bank = ctx.enter_context(nc.psum_tensor("acc_bank", [P, 512], F32))
        misc = ctx.enter_context(nc.psum_tensor("misc", [P, 512], F32))

        ident = sb("ident", [P, P])
        ident_b = sb("ident_b", [P, P], BF16)
        causal = sb("causal", [P, HPG, P], BF16)
        minus_half = sb("minus_half", [P, NT])
        euler = sb("euler", [P, NT])
        expert_idi = sb("expert_idi", [P, NT, E], mybir.dt.int32)
        expert_ids = sb("expert_ids", [P, NT, E])
        wqkv_s = sb("wqkv_s", [P, 3, P])
        bqk_s = sb("bqk_s", [P, 2])
        bv_s = sb("bv_s", [P, P])
        wp_s = sb("wp_s", [P, P])
        bp_s = sb("bp_s", [P, P])
        wg_s = sb("wg_s", [P, E])
        alpha_s = sb("alpha_s", [P, E])
        lnw_s = sb("lnw_s", [P, E])
        lnb_s = sb("lnb_s", [P, E])
        b1_s = sb("b1_s", [P, E * NK])
        b2_s = sb("b2_s", [E, C])
        w1_s = sb("w1_s", [P, E, F])
        w2_s = sb("w2_s", [P, E, NK * C])
        xt = sb("xt", [P, B * NT, C])
        stats = sb("stats", [P, NT, 6])
        mean_var = sb("mean_var", [P, NT, 2])
        var_eps = sb("var_eps", [P, NT])
        rstd = sb("rstd", [P, NT])
        xf = sb("xf", [P, NT, C])
        z = sb("z", [P, NT, C])
        xfT = sb("xfT", [P, T])
        zT_hi = sb("zT_hi", [P, 2, T], F32R)
        zT_lo = sb("zT_lo", [P, 2, T], F32R)
        gate_in = sb("gate_in", [P, NT, E])
        top = sb("top", [P, NT, E])
        top_at = sb("top_at", [P, NT, E], U32)
        top_atf = sb("top_atf", [P, NT, 2])
        diff = sb("diff", [P, NT])
        second = sb("second", [P, NT])
        denom = sb("denom", [P, NT])
        gates = sb("gates", [P, NT, 2])
        pick = sb("pick", [P, 2, NT, E])
        comb = sb("comb", [P, 2, NT, E])
        combT = sb("combT", [E, T])
        sumT = sb("sumT", [P, 2, T])
        comb_dram = nc.dram_tensor("comb_dram", [B, E, T], F32, kind="Internal").ap()
        with ExitStack() as attention:
            def sb_a(name, shape, dt=F32):
                return sb(name, shape, dt, attention)

            stack = [[sb_a(f"stack_{'qk'[i]}{j}", [P, H, T], BF16) for j in range(2)] for i in range(2)]
            v1 = sb_a("v1", [P, 2, NT, H, 32])
            probs = sb_a("probs", [P, P_RING, 512])
            xn = sb_a("xn", [P, NT, C])
            xnT = sb_a("xnT", [P, T])
            qk32 = sb_a("qk32", [P, 2, T])
            parts = sb_a("parts", [P, 2, PARTS, T], BF16)
            row_max = sb_a("row_max", [P, 2, HPG, NT])
            max_parts = sb_a("max_parts", [P, PARTS, NT * HPG], BF16)
            max_rows = sb_a("max_rows", [PARTS * NT * HPG, 2, P], BF16)
            oT = sb_a("oT", [P, 2, T])
            inv_sum = sb_a("inv_sum", [P, NT, HPG])
            on = sb_a("on", [P, NT, C])
            onT = sb_a("onT", [P, T])
        w_parts = [[sb(f"w{i + 1}_{'hi' if not j else 'lo'}", [P, E, F], F32R) for j in range(2)] for i in range(2)]
        hidden = sb("hidden", [P, H_RING, T])
        hidden_hi = sb("hidden_hi", [P, 2, NK, T], F32R)
        hidden_lo = sb("hidden_lo", [P, 2, NK, T], F32R)
        gate_rows = sb("gate_rows", [P, GATE_RING, T])
        scaled = sb("scaled", [P, 2, T])

        s_x = [sem(f"s_x{b}") for b in range(B)]
        s_wqkv, s_wp, s_w1, s_w2, s_small = (sem(n) for n in ("s_wqkv", "s_wp", "s_w1", "s_w2", "s_small"))
        s_pool = sem("s_pool")
        s_ident = sem("s_ident")
        s_vinit = sem("s_vinit")
        s_zero, s_zero1 = sem("s_zero"), sem("s_zero1")
        s_ln = sem("s_ln")
        s_stats = sem("s_stats")
        s_var = sem("s_var")
        s_rstd = sem("s_rstd")
        s_xn, s_xf, s_z = sem("s_xn"), sem("s_xf"), sem("s_z")
        s_fill = sem("s_fill")
        s_free = sem("s_free")
        s_split = sem("s_split")
        s_stack = [[sem(f"s_stack_{'qk'[i]}{j}") for j in range(2)] for i in range(2)]
        s_pass1, s_max = sem("s_pass1"), sem("s_max")
        s_pass2, s_exp = sem("s_pass2"), sem("s_exp")
        s_cut, s_pv = sem("s_cut"), sem("s_pv")
        s_mpart = sem("s_mpart")
        s_mrow = [sem(f"s_mrow{j}") for j in range(2)]
        s_pvout = sem("s_pvout")
        s_inv = sem("s_inv")
        s_resid = sem("s_resid")
        s_w1s = sem("s_w1s")
        s_diff, s_second, s_comb = sem("s_diff"), sem("s_second"), sem("s_comb")
        s_whi, s_wlo = sem("s_whi"), sem("s_wlo")
        s_zhi = sem("s_zhi")
        s_combst = sem("s_combst")
        s_gate = [sem(f"s_gate{j}") for j in range(GATE_RING)]
        s_h, s_gelu = sem("s_h"), sem("s_gelu")
        s_hhi = sem("s_hhi")
        s_hlo, s_hlo_pool = sem("s_hlo"), sem("s_hlo_pool")
        s_y, s_scaled, s_sum = sem("s_y"), sem("s_scaled"), sem("s_sum")
        s_done = sem("s_done")
        s_out = sem("s_out")

        def wait(eng, semaphore, value):
            if value > 0:
                eng.wait_ge(semaphore, value)

        def unit_of(n):
            g, u = divmod(n, UNITS)
            blocks, heads = UNIT[u]
            return g, u, blocks * P, heads

        def columns(n, slot):
            _, _, w, heads = unit_of(n)
            return slots[:, slot, 0:len(heads) * w].rearrange("p (h w) -> p h w", w=w)

        def probs_of(n):
            _, _, w, heads = unit_of(n)
            return probs[:, n % P_RING, 0:len(heads) * w].rearrange("p (h w) -> p h w", w=w)

        def wait_slot(eng, stage):
            i = slot_no[stage]
            if i >= SLOTS:
                kind, n = fills[i - SLOTS]
                wait(eng, s_max if kind == "pass1" else s_exp, n + 1)
            return i % SLOTS

        def wait_filled(eng, stage):
            wait(eng, s_fill, misc_no[stage] + 1)

        def wait_low(eng, j):
            if j >= 0:
                i, k = divmod(j, NK)
                if k == POOL_CHUNK:
                    eng.wait_ge(s_hlo_pool, i + 1)
                else:
                    eng.wait_ge(s_hlo, (NK - 1) * i + k + (k < POOL_CHUNK))

        def fc2_bank(i):
            return acc_bank[:, :] if i % 2 == 0 else slots[:, FC1_SLOTS, :]

        block = ctx.enter_context(nc.Block())

        def walk(handlers, fills_misc=False):
            for s in schedule:
                if s[0] == "read" and not fills_misc:
                    s = s[1]
                elif s[0] in MISC and not fills_misc:
                    continue
                if s[0] in handlers:
                    handlers[s[0]](*s[1:])

        @block.sync
        def _(sp):
            def load_x(b):
                sp.dma_start(xt[:, NT * b:NT * b + NT, :],
                             x[b].rearrange("(n p) c -> p n c", p=P)).then_inc(s_x[b], 16)

            load_x(0)
            for i, w in enumerate((wqT, wkT, wvT)):
                sp.dma_start(wqkv_s[:, i, :], w).then_inc(s_wqkv, 16)
            for i, v in enumerate((bq, bk)):
                sp.dma_start(bqk_s[:, i:i + 1], v.rearrange("(p a) -> p a", a=1)).then_inc(s_wqkv, 16)
            sp.dma_start(bv_s[:, :], bv.rearrange("(a c) -> a c", a=1).broadcast_to([P, C])).then_inc(s_wqkv, 16)
            load_x(1)
            sp.dma_start(wp_s[:, :], wpT).then_inc(s_wp, 16)
            sp.dma_start(bp_s[:, :], bp.rearrange("(a c) -> a c", a=1).broadcast_to([P, C])).then_inc(s_wp, 16)
            sp.dma_start(w1_s[:, :, :], w1.rearrange("e h f -> h e f")).then_inc(s_w1, 16)
            sp.dma_start(lnw_s[:, :], lnwT).then_inc(s_small, 16)
            sp.dma_start(lnb_s[:, :], lnbT).then_inc(s_small, 16)
            sp.dma_start(b1_s[:, :], b1T).then_inc(s_small, 16)
            sp.dma_start(wg_s[:, :], wg).then_inc(s_small, 16)
            sp.dma_start(b2_s[:, :], b2).then_inc(s_small, 16)
            sp.dma_start(alpha_s[:, :], alpha.rearrange("(a c) -> a c", a=1).broadcast_to([P, E])).then_inc(s_small, 16)

            def stack_up(b, i):
                wait(sp, s_split, split_no[("split", b, i, 3)] + 1)
                wait(sp, (s_zero, s_zero1)[b % 2], 1)
                wait(sp, s_pass2, (b - 1) * NG * UNITS)
                for first, count, part, step in (Q_PRODUCTS, K_PRODUCTS)[i]:
                    for j in range(count):
                        r = (first + j) * D
                        sp.dma_start(stack[i][b % 2][r:r + D, :, :], parts[:, i, part + j * step, :])\
                          .then_inc(s_stack[i][b % 2], 16)
                if i == 1 and b == 0:
                    sp.dma_start(w2_s[:, :, :].rearrange("p e (k c) -> p (e k) c", c=C),
                                 w2.rearrange("e (k p) h -> p (e k) h", p=P)).then_inc(s_w2, 16)
                    for later in range(2, B):
                        load_x(later)

            def store_max(g):
                b, hg = divmod(g, NG)
                wait(sp, s_free, misc_no[("maxT", g)] + 1)
                sp.dma_start(stack[0][b % 2][MAX_ROW:K2, HPG * hg:HPG * hg + HPG, :], max_rows[:, g % 2, :])\
                  .then_inc(s_mrow[g % 2], 16)

            def store_comb(b):
                wait(sp, s_free, misc_no[("combT", b)] + 1)
                sp.dma_start(comb_dram[b], combT[:, :]).then_inc(s_combst, 16)

            def load_gates(i):
                b, e = divmod(i, E)
                if i == 0:
                    wait(sp, s_pv, G * NT)
                    wait(sp, s_free, misc_no[("proj", B - 1)] + 1)
                if e == 0:
                    wait(sp, s_combst, 16 * (b + 1))
                wait(sp, s_scaled, i + 1 - GATE_RING)
                sp.dma_start(gate_rows[:, i % GATE_RING, :], comb_dram[b, e:e + 1, :].broadcast_to([P, T]))\
                  .then_inc(s_gate[i % GATE_RING], 16)

            def store(b):
                wait(sp, s_done, b + 1)
                sp.dma_start(out[b].rearrange("(n p) c -> p n c", p=P),
                             xt[:, NT * b:NT * b + NT, :]).then_inc(s_out, 16)

            walk({"stack": stack_up, "maxT": store_max, "combT": store_comb, "gates": load_gates, "outT": store})
            sp.wait_ge(s_out, 16 * B)

        @block.tensor
        def _(pe):
            def claim(stage):
                wait(pe, s_free, misc_no[stage])

            def transpose_tiles(stage, src):
                for n in range(NT):
                    mm = pe.transpose(misc[:, n * P:n * P + P], src[:, n, :], ident[:, :])
                mm.then_inc(s_fill, 1)

            def turn_xn(b):
                claim(("xnT", b))
                if b == 0:
                    pe.wait_ge(s_ident, 1)
                wait(pe, s_xn, b + 1)
                transpose_tiles(("xnT", b), xn)

            def project(b, i, name):
                claim((name, b))
                pe.wait_ge(s_wqkv, 16 * 6)
                pe.matmul(misc[:, :], wqkv_s[:, i, :], xnT[:, :], start=True, stop=True).then_inc(s_fill, 1)

            def project_v(b):
                claim(("v", b))
                for n in range(NT):
                    mm = pe.matmul(misc[:, n * P:n * P + P], xnT[:, n * P:n * P + P], wqkv_s[:, 2, :],
                                   start=True, stop=True)
                mm.then_inc(s_fill, 1)

            def pass1(n):
                g, u, w, heads = unit_of(n)
                b, hg = divmod(g, NG)
                slot = wait_slot(pe, ("pass1", n))
                if n % (NG * UNITS) == 0:
                    for i in range(2):
                        pe.wait_ge(s_stack[i][b % 2], 16 * 6 * (b // 2 + 1))
                cols = columns(n, slot)
                blk = w // P - 1
                q, k = stack[0][b % 2], stack[1][b % 2]
                pe.matmul(cols[:, :, w - P:w], ident_b[:, :], causal[:, 0:len(heads), :],
                          start=True, stop=False, skip_group_check=True)
                for i, h in enumerate(heads):
                    hh = HPG * hg + h
                    mm = pe.matmul(cols[:, i, :], q[0:K1, hh, blk * P:blk * P + P], k[0:K1, hh, 0:w],
                                   start=False, stop=True, skip_group_check=True)
                mm.then_inc(s_pass1, 1)

            def pass2(n):
                g, u, w, heads = unit_of(n)
                b, hg = divmod(g, NG)
                slot = wait_slot(pe, ("pass2", n))
                if u == 0:
                    pe.wait_ge(s_mrow[g % 2], 16 * (g // 2 + 1))
                cols = columns(n, slot)
                blk = NT - w // P
                q, k = stack[0][b % 2], stack[1][b % 2]
                for i, h in enumerate(heads):
                    hh = HPG * hg + h
                    mm = pe.matmul(cols[:, i, :], k[0:K2, hh, blk * P:blk * P + P], q[0:K2, hh, blk * P:T],
                                   start=True, stop=True)
                mm.then_inc(s_pass2, 1)

            def pv(g, row):
                b, hg = divmod(g, NG)
                last = g * UNITS + ROW_END[row]
                wait(pe, s_cut, last + 1)
                if row == 0:
                    wait(pe, s_pvout, g)
                    wait(pe, s_free, misc_no[("v", b)] + 1)
                for h in range(HPG):
                    u = next(u for u in range(UNITS) if UNIT[u][0] == NT - row and h in UNIT[u][1])
                    p = probs_of(g * UNITS + u)[:, h - UNIT[u][1][0], :]
                    mm = pe.matmul(acc_bank[32 * h:32 * h + 32, row * P:T], v1[:, b % 2, row, HPG * hg + h, :],
                                   p, start=(row == 0), stop=(row == NT - 1), tile_position=(0, 32 * h))
                mm.then_inc(s_pv, 1)

            def turn_max(g):
                claim(("maxT", g))
                wait(pe, s_mpart, 4 * (g + 1))
                pe.transpose(misc[:, :].bitcast(BF16)[0:PARTS * NT * HPG, 0:P],
                             max_parts[:, :, :].rearrange("p a m -> p (a m)"), ident_b[:, :]).then_inc(s_fill, 1)

            def turn_o(g):
                claim(("oT", g))
                wait(pe, s_pvout, g + 1)
                for n in range(NT):
                    mm = pe.transpose(misc[:, n * P:n * P + P], oT[:, g % 2, n * P:n * P + P], ident[:, :])
                mm.then_inc(s_fill, 1)

            def turn_on(b):
                claim(("onT", b))
                transpose_tiles(("onT", b), on)

            def project_out(b):
                claim(("proj", b))
                pe.wait_ge(s_wp, 32)
                for n in range(NT):
                    mm = pe.matmul(misc[:, n * P:n * P + P], onT[:, n * P:n * P + P], wp_s[:, :],
                                   start=True, stop=True)
                mm.then_inc(s_fill, 1)

            def hidden_bias(pair):
                claim(("hidden_bias", pair))
                pe.wait_ge(s_w1, 16)
                pe.wait_ge(s_small, 16 * 6)
                for e in range(2 * pair, 2 * pair + 2):
                    for k in range(NK):
                        i = e * NK + k
                        mm = pe.matmul(misc[:, i:i + 1], w1_s[:, e, k * P:k * P + P], lnb_s[:, e:e + 1],
                                       start=True, stop=True)
                mm.then_inc(s_fill, 1)

            def turn_xf(b):
                claim(("xfT", b))
                wait(pe, s_xf, b + 1)
                transpose_tiles(("xfT", b), xf)

            def turn_z(b):
                claim(("zT", b))
                wait(pe, s_z, b + 1)
                transpose_tiles(("zT", b), z)

            def gate(b):
                claim(("gate", b))
                for n in range(NT):
                    mm = pe.matmul(misc[:, n * E:n * E + E], xfT[:, n * P:n * P + P], wg_s[:, :],
                                   start=True, stop=True)
                mm.then_inc(s_fill, 1)

            def turn_comb(b):
                claim(("combT", b))
                wait(pe, s_comb, b + 1)
                for n in range(NT):
                    mm = pe.transpose(misc[0:E, n * P:n * P + P], comb[:, b % 2, n, :], ident[:, :])
                mm.then_inc(s_fill, 1)

            def fc2_bias(b):
                claim(("fc2_bias", b))
                pe.matmul(misc[:, :], b2_s[:, :], combT[:, :], start=True, stop=True).then_inc(s_fill, 1)

            def three_passes(dst, w_hi, w_lo, m_hi, m_lo, first, last):
                pe.matmul(dst, w_hi, m_hi, start=first, stop=False)
                pe.matmul(dst, w_hi, m_lo, start=False, stop=False)
                return pe.matmul(dst, w_lo, m_hi, start=False, stop=last)

            def fc1(i):
                b, e = divmod(i, E)
                if i == 0:
                    wait(pe, s_exp, G * UNITS)
                if b == 0:
                    wait(pe, s_wlo, 2 * e + 2)
                if e == 0:
                    wait(pe, s_free, misc_no[("zT", b)] + 1)
                w_hi, w_lo = w_parts[0]
                for k in range(NK):
                    j = i * NK + k
                    wait(pe, s_gelu, j + 1 - FC1_SLOTS)
                    three_passes(slots[:, j % FC1_SLOTS, :], w_hi[:, e, k * P:k * P + P], w_lo[:, e, k * P:k * P + P],
                                 zT_hi[:, b % 2, :], zT_lo[:, b % 2, :], True, True).then_inc(s_h, 1)

            def fc2(i):
                e = i % E
                if i == 0:
                    wait(pe, s_pvout, G)
                wait(pe, s_scaled, i - 1)
                w_hi, w_lo = w_parts[1]
                for k in range(NK):
                    wait_low(pe, NK * i + k)
                    mm = three_passes(fc2_bank(i), w_hi[:, e, k * C:k * C + C], w_lo[:, e, k * C:k * C + C],
                                      hidden_hi[:, i % 2, k, :], hidden_lo[:, i % 2, k, :], k == 0, k == NK - 1)
                mm.then_inc(s_y, 1)

            def turn_out(b):
                claim(("outT", b))
                wait(pe, s_sum, E * (b + 1))
                for n in range(NT):
                    mm = pe.transpose(misc[:, n * P:n * P + P], sumT[:, b % 2, n * P:n * P + P], ident[:, :])
                mm.then_inc(s_fill, 1)

            walk({"xnT": turn_xn, "q": lambda b: project(b, 0, "q"), "k": lambda b: project(b, 1, "k"),
                  "v": project_v, "pass1": pass1, "pass2": pass2, "pv": pv, "maxT": turn_max, "oT": turn_o,
                  "onT": turn_on, "proj": project_out, "hidden_bias": hidden_bias, "xfT": turn_xf,
                  "zT": turn_z, "gate": gate, "combT": turn_comb, "fc2_bias": fc2_bias, "fc1": fc1, "fc2": fc2,
                  "outT": turn_out}, fills_misc=True)

        @block.scalar
        def _(act):
            def copy_misc(stage, dst):
                wait_filled(act, stage)
                act.activation(dst, misc[:, :], ACT.Copy).then_inc(s_free, 1)

            def turn_xn(b):
                copy_misc(("xnT", b), xnT[:, :])

            def biased(b, i, name):
                wait_filled(act, (name, b))
                if b > 0:
                    wait(act, s_split, split_no[("split", b - 1, i, 3)] + 1)
                act.activation(qk32[:, i, :], misc[:, :], ACT.Identity, bias=bqk_s[:, i:i + 1]).then_inc(s_free, 1)

            def split(b, i, step):
                if step == 0 and b > 0:
                    act.wait_ge(s_stack[i][(b - 1) % 2], 16 * 6 * ((b - 1) // 2 + 1))
                if step == 0:
                    wait(act, s_free, misc_no[(("q", b), ("k", b))[i]] + 1)
                if step % 2 == 0:
                    wait(act, s_split, split_no[("split", b, i, step)])
                    act.activation(parts[:, i, step // 2, :], qk32[:, i, :], ACT.Copy).then_inc(s_split, 1)

            def pass2(n):
                slot = slot_no[("pass2", n)] % SLOTS
                wait(act, s_pass2, n + 1)
                if n >= P_RING:
                    old_g, old_u = divmod(n - P_RING, UNITS)
                    row = next(r for r in range(NT) if old_u <= ROW_END[r])
                    wait(act, s_pv, NT * old_g + row + 1)
                act.activation(probs_of(n), columns(n, slot), ACT.Exp, scale=SCALE).then_inc(s_exp, 1)

            def pv_out(g):
                wait(act, s_pv, NT * (g + 1))
                if g >= 2:
                    wait(act, s_fill, misc_no[("oT", g - 2)] + 1)
                act.activation(oT[:, g % 2, :], acc_bank[:, :], ACT.Copy).then_inc(s_pvout, 1)

            def split_w(e):
                if e == 0:
                    wait(act, s_pass2, G * UNITS)
                    act.wait_ge(s_w2, 16)
                wait(act, s_w1s, e + 1)
                act.activation(w_parts[0][0][:, e, :], w1_s[:, e, :], ACT.Copy).then_inc(s_whi, 1)
                act.activation(w_parts[1][0][:, e, :], w2_s[:, e, :], ACT.Copy).then_inc(s_whi, 1)

            def turn_z(b):
                wait_filled(act, ("zT", b))
                if b >= 2:
                    wait(act, s_h, NK * E * (b - 1))
                act.activation(zT_hi[:, b % 2, :], misc[:, :], ACT.Copy).then_inc(s_zhi, 1)

            def fc1(i):
                b, e = divmod(i, E)
                if i == 0:
                    wait(act, s_pv, G * NT)
                wait(act, s_y, i - 1)
                for k in range(NK):
                    j = i * NK + k
                    wait(act, s_h, j + 1)
                    wait_low(act, j - H_RING)
                    if k % 2 == 0:
                        act.activation(hidden_hi[:, i % 2, k, :], slots[:, j % FC1_SLOTS, :], ACT.Gelu_apprx_tanh,
                                       bias=b1_s[:, e * NK + k:e * NK + k + 1])
                    act.activation(hidden[:, j % H_RING, :], slots[:, j % FC1_SLOTS, :], ACT.Gelu_apprx_tanh,
                                   bias=b1_s[:, e * NK + k:e * NK + k + 1]).then_inc(s_gelu, 1)

            def turn_comb(b):
                wait_filled(act, ("combT", b))
                wait(act, s_combst, 16 * b)
                act.activation(combT[:, :], misc[0:E, :], ACT.Copy).then_inc(s_free, 1)

            walk({"xnT": turn_xn, "q": lambda b: biased(b, 0, "q"), "k": lambda b: biased(b, 1, "k"),
                  "split": split, "pass2": pass2, "pv_out": pv_out, "onT": lambda b: copy_misc(("onT", b), onT[:, :]),
                  "xfT": lambda b: copy_misc(("xfT", b), xfT[:, :]),
                  "zT": turn_z, "split_w": split_w,
                  "combT": turn_comb, "fc1": fc1})

        @block.vector
        def _(dve):
            chain = [0]

            def link(ins):
                ins.then_inc(s_ln, 1)
                chain[0] += 1
                dve.wait_ge(s_ln, chain[0])

            minus_ones = float(np.array([0xBF80BF80], np.uint32).view(np.float32)[0])
            for i in range(2):
                dve.memset(stack[i][0][0:MAX_ROW, :, :].bitcast(F32), 0.0)
            dve.memset(stack[1][0][MAX_ROW:K2, :, :].bitcast(F32), minus_ones).then_inc(s_zero, 1)
            stats_no, variance_no = [0], [0]

            def variance(src):
                for n in range(NT):
                    last = dve.bn_stats(stats[:, n, :], src[:, n, :])
                last.then_inc(s_stats, 1)
                stats_no[0] += 1

            def aggregate(*_):
                dve.wait_ge(s_stats, stats_no[0])
                for n in range(NT):
                    last = dve.bn_aggr(mean_var[:, n, :], stats[:, n, :])
                link(last)
                dve.tensor_scalar(var_eps[:, :], mean_var[:, :, 1], EPS, None, ALU.add).then_inc(s_var, 1)
                variance_no[0] += 1

            def normalise(dst, src):
                wait(dve, s_rstd, variance_no[0])
                for n in range(NT):
                    last = dve.tensor_scalar(dst[:, n, :], src[:, n, :], mean_var[:, n, 0:1], rstd[:, n:n + 1],
                                             ALU.subtract, ALU.mult)
                return last

            def ln_stats(b):
                dve.wait_ge(s_x[b], 16)
                variance(xt[:, NT * b:NT * b + NT, :])

            def ln_apply(b):
                if b > 0:
                    wait_filled(dve, ("xnT", b - 1))
                normalise(xn, xt[:, NT * b:NT * b + NT, :]).then_inc(s_xn, 1)

            def put_v(b):
                wait_filled(dve, ("v", b))
                if b == 0:
                    dve.wait_ge(s_vinit, 1)
                wait(dve, s_pv, (b - 1) * NG * NT)
                dve.tensor_tensor(v1[:, b % 2, :, :, 0:D],
                                  misc[:, :].rearrange("p (n h d) -> p n h d", h=H, d=D),
                                  bv_s[:, :].rearrange("p (a h d) -> p a h d", a=1, h=H)
                                  .broadcast_to([P, NT, H, D]), ALU.add).then_inc(s_free, 1)

            def pass1(n):
                g, u, w, heads = unit_of(n)
                slot = slot_no[("pass1", n)] % SLOTS
                wait(dve, s_pass1, n + 1)
                if u == 0 and g >= 2:
                    wait(dve, s_mpart, 4 * (g - 1))
                dve.tensor_reduce(row_max[:, g % 2, heads[0]:heads[-1] + 1, w // P - 1], columns(n, slot), AX.X, ALU.max)\
                   .then_inc(s_max, 1)

            def turn_max(g):
                wait_filled(dve, ("maxT", g))
                if g >= 2:
                    dve.wait_ge(s_mrow[g % 2], 16 * (g // 2))
                dve.tensor_copy(max_rows[:, g % 2, :], misc[:, :].bitcast(BF16)[0:PARTS * NT * HPG, 0:P])\
                   .then_inc(s_free, 1)

            def turn_o(g):
                b, hg = divmod(g, NG)
                wait_filled(dve, ("oT", g))
                o = misc[:, :].rearrange("p (n h d) -> p n h d", h=HPG, d=32)
                dve.reciprocal(inv_sum[:, :, :], o[:, :, :, D]).then_inc(s_inv, 1)
                dve.wait_ge(s_inv, g + 1)
                if hg == 0 and b > 0:
                    wait_filled(dve, ("onT", b - 1))
                dst = on[:, :, HPG * D * hg:HPG * D * (hg + 1)].rearrange("p n (h d) -> p n h d", d=D)
                scale = inv_sum[:, :, :].rearrange("p n (h a) -> p n h a", a=1).broadcast_to([P, NT, HPG, D])
                dve.tensor_tensor(dst, o[:, :, :, 0:D], scale, ALU.mult).then_inc(s_free, 1)

            def project_out(b):
                wait_filled(dve, ("proj", b))
                wait(dve, s_resid, b + 1)
                tile = xt[:, NT * b:NT * b + NT, :]
                dve.tensor_tensor(tile, misc[:, :].rearrange("p (n c) -> p n c", c=C), tile, ALU.add)\
                   .then_inc(s_free, 1)

            def hidden_bias(pair):
                wait_filled(dve, ("hidden_bias", pair))
                cols = slice(2 * NK * pair, 2 * NK * (pair + 1))
                dve.tensor_tensor(b1_s[:, cols], misc[:, cols], b1_s[:, cols], ALU.add).then_inc(s_free, 1)

            def scale_w1(e):
                wait(dve, s_free, misc_no[("hidden_bias", e // 2)] + 1)
                dve.tensor_scalar(w1_s[:, e, :], w1_s[:, e, :], lnw_s[:, e:e + 1], None, ALU.mult)\
                   .then_inc(s_w1s, 1)

            def stats1(b):
                wait(dve, s_free, misc_no[("proj", b)] + 1)
                variance(xt[:, NT * b:NT * b + NT, :])

            def make_xf(b):
                if b > 0:
                    wait_filled(dve, ("xfT", b - 1))
                normalise(xf, xt[:, NT * b:NT * b + NT, :]).then_inc(s_xf, 1)

            def stats2(b):
                dve.wait_ge(s_xf, b + 1)
                variance(xf)

            def make_z(b):
                if b > 0:
                    wait_filled(dve, ("zT", b - 1))
                normalise(z, xf).then_inc(s_z, 1)

            def gate(b):
                wait_filled(dve, ("gate", b))
                dve.tensor_copy(gate_in[:, :, :], misc[:, 0:NT * E].rearrange("p (n e) -> p n e", e=E))\
                   .then_inc(s_free, 1)

            def top_two(b):
                wait(dve, s_free, misc_no[("gate", b)] + 1)
                for n in range(NT):
                    last = dve.max(top[:, n, :], gate_in[:, n, :])
                link(last)
                for n in range(NT):
                    last = dve.max_index(top_at[:, n, :], top[:, n, :], gate_in[:, n, :])
                link(last)
                wait(dve, s_second, b)
                dve.tensor_tensor(diff[:, :], top[:, :, 1], top[:, :, 0], ALU.subtract).then_inc(s_diff, 1)
                link(dve.tensor_copy(top_atf[:, :, :], top_at[:, :, 0:2]))
                for j in range(2):
                    last = dve.tensor_tensor(pick[:, j, :, :], expert_ids[:, :, :],
                                             top_atf[:, :, j:j + 1].broadcast_to([P, NT, E]), ALU.is_equal)
                link(last)

            def combine(b):
                wait(dve, s_second, b + 1)
                link(dve.tensor_scalar(denom[:, :], second[:, :], 1.0, None, ALU.add))
                link(dve.reciprocal(gates[:, :, 0], denom[:, :]))
                link(dve.tensor_tensor(gates[:, :, 1], gates[:, :, 0], second[:, :], ALU.mult))
                for j in range(2):
                    last = dve.tensor_tensor(pick[:, j, :, :], pick[:, j, :, :],
                                             gates[:, :, j:j + 1].broadcast_to([P, NT, E]), ALU.mult)
                link(last)
                link(dve.tensor_tensor(pick[:, 0, :, :], pick[:, 0, :, :], pick[:, 1, :, :], ALU.add))
                dve.tensor_tensor(comb[:, b % 2, :, :], pick[:, 0, :, :],
                                  alpha_s[:, :].rearrange("p (a e) -> p a e", a=1).broadcast_to([P, NT, E]),
                                  ALU.mult).then_inc(s_comb, 1)

            def turn_z(b):
                wait(dve, s_zhi, b + 1)
                dve.tensor_tensor(zT_lo[:, b % 2, :], misc[:, :], zT_hi[:, b % 2, :].bitcast(F32), ALU.subtract)\
                   .then_inc(s_free, 1)

            def fc2_bias(b):
                wait_filled(dve, ("fc2_bias", b))
                dve.tensor_copy(sumT[:, b % 2, :], misc[:, :]).then_inc(s_free, 1)

            def fc1(i):
                wait(dve, s_y, i - 1)
                for k in range(NK):
                    if k == POOL_CHUNK:
                        continue
                    j = i * NK + k
                    wait(dve, s_gelu, j + 1)
                    if k % 2 == 1:
                        dve.tensor_copy(hidden_hi[:, i % 2, k, :], hidden[:, j % H_RING, :]).then_inc(s_hhi, 1)
                        dve.wait_ge(s_hhi, (j + 1) // 2)
                    dve.tensor_tensor(hidden_lo[:, i % 2, k, :], hidden[:, j % H_RING, :],
                                      hidden_hi[:, i % 2, k, :].bitcast(F32), ALU.subtract).then_inc(s_hlo, 1)

            def fc2(i):
                wait(dve, s_y, i + 1)
                dve.wait_ge(s_gate[i % GATE_RING], 16 * (i // GATE_RING + 1))
                wait(dve, s_sum, i - 1)
                dve.tensor_tensor(scaled[:, i % 2, :], fc2_bank(i), gate_rows[:, i % GATE_RING, :], ALU.mult)\
                   .then_inc(s_scaled, 1)

            def turn_out(b):
                wait_filled(dve, ("outT", b))
                tile = xt[:, NT * b:NT * b + NT, :]
                dve.tensor_tensor(tile, misc[:, :].rearrange("p (n c) -> p n c", c=C), tile, ALU.add)\
                   .then_inc(s_done, 1)
                dve.sem_inc(s_free, 1)

            walk({"ln_stats": ln_stats, "ln_apply": ln_apply, "v": put_v, "pass1": pass1, "maxT": turn_max,
                  "oT": turn_o, "proj": project_out, "hidden_bias": hidden_bias, "scale_w1": scale_w1, "r_stats1": stats1,
                  "ln_agg": aggregate, "r_agg1": aggregate, "r_agg2": aggregate, "r_stats2": stats2, "r_xf": make_xf, "r_z": make_z, "gate": gate, "r_top": top_two, "r_comb": combine,
                  "zT": turn_z, "fc2_bias": fc2_bias, "fc1": fc1, "fc2": fc2, "outT": turn_out})

        @block.gpsimd
        def _(pool):
            steps = [0]

            def link(ins):
                ins.then_inc(s_pool, 1)
                steps[0] += 1
                pool.wait_ge(s_pool, steps[0])

            link(pool.memset(minus_half[:, :], -0.5))
            link(pool.memset(euler[:, :], math.e))
            link(pool.memset(ident[:, :], 0.0))
            link(pool.affine_select(out=ident[:, :], in_=ident[:, :], compare_op=ALU.not_equal, fill=1.0,
                                    base=0, pattern=[[-1, P]], channel_multiplier=1))
            link(pool.tensor_copy(ident_b[:, :], ident[:, :]))
            link(pool.memset(causal[:, :, :], 0.0))
            pool.affine_select(out=causal[:, :, :], in_=causal[:, :, :], compare_op=ALU.is_ge, fill=NEG,
                               base=0, pattern=[[0, HPG], [-1, P]], channel_multiplier=1).then_inc(s_ident, 1)
            variance_no = [0]

            def rsqrt(*_):
                variance_no[0] += 1
                wait(pool, s_var, variance_no[0])
                pool.tensor_tensor(rstd[:, :], var_eps[:, :], minus_half[:, :], ALU.pow).then_inc(s_rstd, 1)

            def second_gate(b):
                wait(pool, s_diff, b + 1)
                pool.tensor_tensor(second[:, :], euler[:, :], diff[:, :], ALU.pow).then_inc(s_second, 1)

            def init_v(*_):
                link(pool.memset(v1[:, :, :, :, :].rearrange("p i n h d -> p (i n h) d"), 0.0))
                pool.memset(v1[:, :, :, :, D:D + 1].rearrange("p i n h d -> p (i n h) d"), 1.0).then_inc(s_vinit, 1)
                pool.wait_ge(s_vinit, 1)

            def init_stacks(*_):
                minus_ones = float(np.array([0xBF80BF80], np.uint32).view(np.float32)[0])
                for i in range(2):
                    link(pool.memset(stack[i][1][0:MAX_ROW, :, :].bitcast(F32), 0.0))
                pool.memset(stack[1][1][MAX_ROW:K2, :, :].bitcast(F32), minus_ones).then_inc(s_zero1, 1)
                pool.wait_ge(s_zero1, 1)
                link(pool.iota(expert_idi[:, :, :], pattern=[[0, NT], [1, E]], base=0, channel_multiplier=0))
                link(pool.tensor_copy(expert_ids[:, :, :], expert_idi[:, :, :]))

            def split(b, i, step):
                if step % 2 == 1:
                    wait(pool, s_split, split_no[("split", b, i, step)])
                    dst = qk32[:, i, :] if step == 1 else parts[:, i, 2, :]
                    pool.tensor_tensor(dst, qk32[:, i, :], parts[:, i, step // 2, :], ALU.subtract)\
                        .then_inc(s_split, 1)

            def pass2(n):
                g, u, w, heads = unit_of(n)
                wait(pool, s_exp, n + 1)
                diag = probs_of(n)[:, :, 0:P]
                pool.affine_select(out=diag, in_=diag, compare_op=ALU.is_ge, fill=0.0, base=0,
                                   pattern=[[0, len(heads)], [1, P]], channel_multiplier=-1).then_inc(s_cut, 1)

            def split_max(g):
                wait(pool, s_max, UNITS * (g + 1))
                if g > 0:
                    wait_filled(pool, ("maxT", g - 1))
                source = row_max[:, g % 2, :, :].rearrange("p h n -> p (h n)")
                for step in range(4):
                    part = max_parts[:, (step + 1) // 2, :]
                    if step % 2 == 0:
                        ins = pool.tensor_copy(part, source)
                    else:
                        dst = source if step == 1 else part
                        ins = pool.tensor_tensor(dst, source, max_parts[:, step // 2, :], ALU.subtract)
                    ins.then_inc(s_mpart, 1)
                    pool.wait_ge(s_mpart, 4 * g + step + 1)

            def residual(b):
                wait(pool, s_xn, b + 1)
                pool.wait_ge(s_wp, 32)
                tile = xt[:, NT * b:NT * b + NT, :]
                pool.tensor_tensor(tile, tile, bp_s[:, :].rearrange("p (a c) -> p a c", a=1)
                                   .broadcast_to([P, NT, C]), ALU.add).then_inc(s_resid, 1)

            def split_w(e):
                for i, w in enumerate((w1_s, w2_s)):
                    wait(pool, s_whi, 2 * e + i + 1)
                    pool.tensor_tensor(w_parts[i][1][:, e, :], w[:, e, :], w_parts[i][0][:, e, :].bitcast(F32),
                                       ALU.subtract).then_inc(s_wlo, 1)

            def fc1(i):
                wait(pool, s_y, i - 1)
                j = i * NK + POOL_CHUNK
                wait(pool, s_gelu, j + 1)
                pool.tensor_tensor(hidden_lo[:, i % 2, POOL_CHUNK, :], hidden[:, j % H_RING, :],
                                   hidden_hi[:, i % 2, POOL_CHUNK, :].bitcast(F32), ALU.subtract)\
                    .then_inc(s_hlo_pool, 1)

            def fc2(i):
                b = i // E
                if i % E == 0:
                    wait(pool, s_free, misc_no[("fc2_bias", b)] + 1)
                wait(pool, s_scaled, i + 1)
                wait(pool, s_sum, i)
                pool.tensor_tensor(sumT[:, b % 2, :], sumT[:, b % 2, :], scaled[:, i % 2, :], ALU.add)\
                    .then_inc(s_sum, 1)

            walk({"split_w": split_w, "fc1": fc1, "fc2": fc2, "ln_agg": rsqrt, "r_agg1": rsqrt, "r_agg2": rsqrt, "init_v": init_v, "r_exp": second_gate,
                  "init_stacks": init_stacks, "split": split, "pass2": pass2, "max_parts": split_max,
                  "residual": residual})


NAMES = ("x", "wqT", "wkT", "wvT", "bq", "bk", "bv", "wpT", "bp", "wg", "alpha", "lnwT", "lnbT",
         "w1", "b1T", "w2", "b2")


def kernel(L0_attn_x, L0_attn_W_qkv, L0_attn_b_qkv, L0_attn_W_proj, L0_attn_b_proj, L0_ffn_Wg, L0_ffn_alpha,
           L0_ffn_ln_w, L0_ffn_ln_b, L0_ffn_fc1_w, L0_ffn_fc1_b, L0_ffn_fc2_w, L0_ffn_fc2_b):
    import numpy as _np
    import concourse.bacc as _bacc
    from concourse import mybir as _mybir
    from concourse.bass_utils import run_bass_kernel_spmd as _run

    w_qkv, b_qkv = _np.asarray(L0_attn_W_qkv), _np.asarray(L0_attn_b_qkv)
    C = w_qkv.shape[1]
    E, F = _np.shape(L0_ffn_fc1_b)
    b1 = _np.asarray(L0_ffn_fc1_b).reshape(E, F // C, C).transpose(2, 0, 1).reshape(C, E * (F // C))
    wq, wk = (w_qkv[i * C:i * C + C].reshape(16, C // 16, C).transpose(1, 0, 2).reshape(C, C) for i in range(2))
    bq, bk = (b_qkv[i * C:i * C + C].reshape(16, C // 16).T.reshape(C) for i in range(2))
    values = (
        L0_attn_x, wq.T, wk.T, w_qkv[2 * C:3 * C].T, bq, bk, b_qkv[2 * C:3 * C],
        _np.asarray(L0_attn_W_proj).T, L0_attn_b_proj, L0_ffn_Wg, L0_ffn_alpha,
        _np.asarray(L0_ffn_ln_w).T, _np.asarray(L0_ffn_ln_b).T, L0_ffn_fc1_w, b1, L0_ffn_fc2_w, L0_ffn_fc2_b,
    )
    nc = _bacc.Bacc("TRN2", target_bir_lowering=False, num_devices=1)
    arrays, args = {}, []
    for name, value in zip(NAMES, values):
        a = _np.ascontiguousarray(value)
        arrays[f"in_{name}"] = a
        args.append(nc.dram_tensor(f"in_{name}", a.shape, _mybir.dt.from_np(a.dtype), kind="ExternalInput").ap())
    out = nc.dram_tensor("out", arrays["in_x"].shape, _mybir.dt.float32, kind="ExternalOutput").ap()
    build(nc, *args, out)
    r = _run(nc, [arrays], core_ids=[0])
    return r.results[0]["out"]
```

```python
import math
from contextlib import ExitStack

import numpy as np

import concourse.bass as bass
from concourse import mybir

F32, F32R, BF16, U32 = mybir.dt.float32, mybir.dt.float32r, mybir.dt.bfloat16, mybir.dt.uint32
ALU = mybir.AluOpType
ACT = mybir.ActivationFunctionType
AX = mybir.AxisListType

P = 128
EPS = 1e-5
NEG = -3.0e38
PARTS = 3
PART_STEP = (0, 2, 3)
STACKED = ((0, 0, 0, 1, 1, 2), (0, 1, 2, 0, 1, 0))
PRODUCTS = len(STACKED[0])
MAX_ROW = 96
K1, K2 = MAX_ROW, MAX_ROW + PARTS
HPG = 4
BANKFUL = ((4, 1), (3, 1), (2, 2), (1, 4))
UNIT = tuple((blocks, tuple(range(h, h + n))) for blocks, n in BANKFUL for h in range(0, HPG, n))
UNITS = len(UNIT)
ROW_END = tuple(max(u for u in range(UNITS) if UNIT[u][0] == blocks) for blocks in (4, 3, 2, 1))
PV_ORDER = tuple(sorted(range(len(ROW_END)), key=lambda row: ROW_END[row]))
LAG = 22
PV_LAG = 7
FRONT = {"ln_stats": 3, "ln_agg": 7, "xnT": 14, "q": 19, "k": 24, "v": 35}
APPLY = (11, 11, 11, 11)
SPLIT = ((20, 21, 24, 30), (32, 33, 35, 36))
GROUP = {"max_parts": 11, "maxT": 16}
BACK = {"residual": 25, "o_load": 42, "o_invert": 50, "o_spread": 57, "o_scale": 61,
        "proj": 64}
HIDDEN_BIAS = (45, 53, 92, 101)
SCALE_W1, SPLIT_W1 = 205, 29
ROUTE = (("r_stats1", 102), ("r_agg1", 108), ("r_xf", 112), ("r_stats2", 115), ("r_agg2", 120), ("r_z", 129),
         ("xfT", 133), ("zT", 143), ("gate", 174), ("r_top", 194), ("r_exp", 197), ("r_comb", 201), ("combT", 222))
SLOTS = 6
P_RING = 12
FC1_SLOTS = SLOTS - 1
POOL_CHUNK = 2
H_RING = 4
GATE_RING = 4


def build(nc, x, wqT, wkT, wvT, bq, bk, bv, wpT, bp, wg, alpha, lnwT, lnbT, w1, b1T, w2, b2T, out):
    B, T, C = x.shape
    E, F = w1.shape[0], w1.shape[2]
    D = 8
    H = C // D
    NT = T // P
    NG = H // HPG
    G = B * NG
    NK = F // P
    SCALE = float(D) ** -0.5

    extra = {}

    def at(n, *stage):
        extra.setdefault(n, []).append(stage)

    for b in range(1, B):
        n = NG * UNITS * (b - 1)
        for name in FRONT:
            at(n + FRONT[name], name, b)
        for tile in range(NT):
            at(n + APPLY[tile], "ln_apply", b, tile)
        for i in range(2):
            for step in range(4):
                at(n + SPLIT[i][step], "split", b, i, step)
                if step in PART_STEP:
                    at(n + SPLIT[i][step], "stack", b, i, PART_STEP.index(step))
    for g in range(G):
        n = g * UNITS
        for name in GROUP:
            at(n + GROUP[name], name, g)
        at(n + LAG + UNITS + PV_LAG, "pv_out", g)
        at(n + LAG + UNITS + PV_LAG, "o_store", g)
        if g % NG == NG - 1:
            for name in BACK:
                if g < G - 1 or name == "residual":
                    at(n + BACK[name], name, g // NG)
    for i in range(E // 2):
        at(HIDDEN_BIAS[i], "hidden_bias", i)
    for e in range(E):
        at(SCALE_W1 + UNITS * e, "scale_w1", e)
    for e in range(NG):
        at((G - NG + e) * UNITS + SPLIT_W1, "split_w1", e)
    at(4, "init_ones")
    at(5, "init_second")
    at(14, "init_experts")
    for name, n in ROUTE:
        at(n, name, 0)

    MISC = ("xnT", "q", "k", "v", "maxT", "proj", "hidden_bias",
            "xfT", "zT", "gate", "combT", "outT")
    schedule, unread = [], []

    def read_misc():
        while unread:
            schedule.append(("read", unread.pop()))

    def add(*stages):
        for s in stages:
            if s[0] in MISC:
                read_misc()
                unread.append(s)
            schedule.append(s)

    add(("ln_stats", 0), ("ln_agg", 0), ("init_zeros",), *(("ln_apply", 0, n) for n in range(NT)),
        ("xnT", 0), ("q", 0))
    read_misc()
    add(("split", 0, 0, 0), ("stack", 0, 0, 0), ("k", 0), ("split", 0, 0, 1), ("split", 0, 0, 2),
        ("stack", 0, 0, 1))
    read_misc()
    add(("split", 0, 1, 0), ("stack", 0, 1, 0), ("split", 0, 0, 3), ("stack", 0, 0, 2), ("split", 0, 1, 1),
        ("split", 0, 1, 2), ("stack", 0, 1, 1), ("split", 0, 1, 3), ("stack", 0, 1, 2), ("init_v",), ("v", 0))
    END = G * UNITS + LAG
    for n in range(END + PV_LAG + 1):
        read_misc()
        if n == END:
            add(("split_w2", 0), ("fc1", 0))
        if n < G * UNITS:
            add(("pass1", n))
        if 0 <= n - LAG < G * UNITS:
            add(("pass2", n - LAG))
        pg, pu = divmod(n - LAG - PV_LAG, UNITS)
        if 0 <= pg < G and pu in ROW_END:
            add(("pv", pg, ROW_END.index(pu)))
        add(*extra.pop(n, []))
    assert not extra
    AHEAD = {(0, 0): ("r_stats1", "r_agg1"), (1, 0): ("r_xf",), (1, 1): ("r_stats2", "r_agg2"),
             (2, 0): ("xfT",), (2, 1): ("r_z",), (3, 0): ("gate",), (3, 1): ("r_top",), (4, 0): ("zT",),
             (4, 1): ("r_exp",), (5, 0): ("r_comb",), (6, 0): ("combT",)}
    LAST = {(2, 0): ("o_load", B - 1), (3, 1): ("o_invert", B - 1), (5, 1): ("o_spread", B - 1), (6, 1): ("o_scale", B - 1),
            (8, 0): ("proj", B - 1)}
    for i in range(1, B * E + 2):
        if i < B * E:
            add(("fc1", i))
        if i < E:
            add(("split_w2", i))
            if i + 3 in range(NG, E):
                add(("split_w1", i + 3))
        b, e = divmod(i - 1, E)
        for place in range(2):
            read_misc()
            if (i, place) in LAST:
                add(LAST[i, place])
            if b + 1 < B:
                add(*((r, b + 1) for r in AHEAD.get((e, place), ())))
            if place == 0:
                if i == 1:
                    add(("gates", 0))
                if i < B * E:
                    add(("gates", i))
                if i <= B * E:
                    add(("fc2", i - 1))
        if e == 0 and b > 0:
            add(("outT", b - 1))
    read_misc()

    misc_no = {}
    for s in schedule:
        if s[0] in MISC:
            misc_no[s] = len(misc_no)
    fills = [s for s in schedule if s[0] in ("pass1", "pass2")]
    slot_no = {s: i for i, s in enumerate(fills)}
    first_bank = len(fills) % SLOTS
    split_no = {}
    for s in schedule:
        if s[0] == "split":
            split_no[s] = len(split_no)

    with ExitStack() as ctx:
        def sb(name, shape, dt=F32, life=ctx):
            return life.enter_context(nc.sbuf_tensor(name, shape, dt))

        def sem(name):
            return ctx.enter_context(nc.semaphore(name))

        slots = ctx.enter_context(nc.psum_tensor("slots", [P, SLOTS, 512], F32))
        acc_bank = ctx.enter_context(nc.psum_tensor("acc_bank", [P, 512], F32))
        misc = ctx.enter_context(nc.psum_tensor("misc", [P, 512], F32))

        ident = sb("ident", [P, P])
        ident_b = sb("ident_b", [P, P], BF16)
        causal = sb("causal", [P, HPG, P], BF16)
        minus_half = sb("minus_half", [P, NT])
        euler = sb("euler", [P, NT])
        expert_idi = sb("expert_idi", [P, NT, E], mybir.dt.int32)
        expert_ids = sb("expert_ids", [P, NT, E])
        wqkv_s = sb("wqkv_s", [P, 3, P])
        bqk_s = sb("bqk_s", [P, 2])
        bv_s = sb("bv_s", [P, P])
        wp_s = sb("wp_s", [P, P])
        bp_s = sb("bp_s", [P, P])
        wg_s = sb("wg_s", [P, E])
        alpha_s = sb("alpha_s", [P, E])
        lnw_s = sb("lnw_s", [P, E])
        lnb_s = sb("lnb_s", [P, E])
        b1_s = sb("b1_s", [P, E * NK])
        b2_s = sb("b2_s", [P, E])
        w1_s = sb("w1_s", [P, E, F])
        w2_s = sb("w2_s", [P, E, NK * C])
        xt = sb("xt", [P, B * NT, C])
        stats = sb("stats", [P, NT, 6])
        mean_var = sb("mean_var", [P, NT, 2])
        var_eps = sb("var_eps", [P, NT])
        rstd = sb("rstd", [P, NT])
        xf = sb("xf", [P, NT, C])
        z = sb("z", [P, NT, C])
        xfT = sb("xfT", [P, T])
        zT_hi = sb("zT_hi", [P, 2, T], F32R)
        zT_lo = sb("zT_lo", [P, 2, T], F32R)
        gate_in = sb("gate_in", [P, NT, E])
        top = sb("top", [P, NT, E])
        top_at = sb("top_at", [P, NT, E], U32)
        top_atf = sb("top_atf", [P, NT, 2])
        diff = sb("diff", [P, NT])
        second = sb("second", [P, NT])
        denom = sb("denom", [P, NT])
        gates = sb("gates", [P, NT, 2])
        pick = sb("pick", [P, 2, NT, E])
        comb = sb("comb", [P, 2, NT, E])
        combT = sb("combT", [E, T])
        sumT = sb("sumT", [P, 2, T])
        o_dram = nc.dram_tensor("o_dram", [B, NG, P, T], F32, kind="Internal").ap()
        inv_dram = nc.dram_tensor("inv_dram", [B, H, T], F32, kind="Internal").ap()
        comb_dram = nc.dram_tensor("comb_dram", [B, E, T], F32, kind="Internal").ap()
        with ExitStack() as attention:
            def sb_a(name, shape, dt=F32):
                return sb(name, shape, dt, attention)

            stack = [list(s) for s in zip(*([sb_a(f"stack_{'qk'[i]}{j}", [P, H, T], BF16) for i in range(2)]
                                            for j in range(2)))]
            v1 = sb_a("v1", [P, 2, NT, H, 32])
            probs = sb_a("probs", [P, P_RING, 512])
            xn = sb_a("xn", [P, NT, C])
            xnT = sb_a("xnT", [P, T])
            qk32 = sb_a("qk32", [P, 2, T])
            parts = sb_a("parts", [P, 2, PARTS, T], BF16)
            row_max = sb_a("row_max", [P, 2, HPG, NT])
            max_parts = sb_a("max_parts", [P, PARTS, NT * HPG], BF16)
            max_rows = sb_a("max_rows", [PARTS * NT * HPG, 2, P], BF16)
            oT = sb_a("oT", [P, 2, T])
            onT = sb_a("onT", [P, T])
            sums = sb_a("sums", [P, H * T // P])
            o_inv = sb_a("o_inv", [P, T])
        w_parts = [[sb(f"w{i + 1}_{'hi' if not j else 'lo'}", [P, E, F], F32R) for j in range(2)] for i in range(2)]
        hidden = sb("hidden", [P, H_RING, T])
        hidden_hi = sb("hidden_hi", [P, 2, NK, T], F32R)
        hidden_lo = sb("hidden_lo", [P, 2, NK, T], F32R)
        gate_rows = sb("gate_rows", [P, GATE_RING, T])
        scaled = sb("scaled", [P, 2, T])

        s_x = [sem(f"s_x{b}") for b in range(B)]
        s_wqkv, s_wp, s_w1, s_w2, s_small = (sem(n) for n in ("s_wqkv", "s_wp", "s_w1", "s_w2", "s_small"))
        s_pool = sem("s_pool")
        s_ident = sem("s_ident")
        s_vinit = sem("s_vinit")
        s_zero = [sem(f"s_zero{j}") for j in range(2)]
        s_minus = [sem(f"s_minus{j}") for j in range(2)]
        s_ids = sem("s_ids")
        s_ln = sem("s_ln")
        s_stats = sem("s_stats")
        s_var = sem("s_var")
        s_rstd = sem("s_rstd")
        s_xn, s_xf, s_z = sem("s_xn"), sem("s_xf"), sem("s_z")
        s_fill = sem("s_fill")
        s_free = sem("s_free")
        s_split = sem("s_split")
        s_stack = [[sem(f"s_stack_{'qk'[i]}{j}") for j in range(2)] for i in range(2)]
        s_pass1, s_max = sem("s_pass1"), sem("s_max")
        s_pass2, s_exp = sem("s_pass2"), sem("s_exp")
        s_cut, s_pv = sem("s_cut"), sem("s_pv")
        s_mpart = sem("s_mpart")
        s_mrow = [sem(f"s_mrow{j}") for j in range(2)]
        s_pvout = sem("s_pvout")
        s_ostore = [sem(f"s_ostore{j}") for j in range(2)]
        s_oload, s_sums = sem("s_oload"), sem("s_sums")
        s_inv = sem("s_inv")
        s_invst, s_invload = sem("s_invst"), sem("s_invload")
        s_on = sem("s_on")
        s_resid = sem("s_resid")
        s_w1s = sem("s_w1s")
        s_diff, s_second, s_comb = sem("s_diff"), sem("s_second"), sem("s_comb")
        s_w1hi, s_w1lo = sem("s_w1hi"), sem("s_w1lo")
        s_w2hi, s_w2lo = sem("s_w2hi"), sem("s_w2lo")
        s_zhi = sem("s_zhi")
        s_combst = sem("s_combst")
        s_gate = [sem(f"s_gate{j}") for j in range(GATE_RING)]
        s_h, s_gelu = sem("s_h"), sem("s_gelu")
        s_hhi = sem("s_hhi")
        s_hlo, s_hlo_pool = sem("s_hlo"), sem("s_hlo_pool")
        s_y, s_scaled, s_sum = sem("s_y"), sem("s_scaled"), sem("s_sum")
        s_done = sem("s_done")
        s_out = sem("s_out")

        def wait(eng, semaphore, value):
            if value > 0:
                eng.wait_ge(semaphore, value)

        def unit_of(n):
            g, u = divmod(n, UNITS)
            blocks, heads = UNIT[u]
            return g, u, blocks * P, heads

        def columns(n, slot):
            _, _, w, heads = unit_of(n)
            return slots[:, slot, 0:len(heads) * w].rearrange("p (h w) -> p h w", w=w)

        def probs_of(n):
            _, _, w, heads = unit_of(n)
            return probs[:, n % P_RING, 0:len(heads) * w].rearrange("p (h w) -> p h w", w=w)

        def wait_slot(eng, stage):
            i = slot_no[stage]
            if i >= SLOTS:
                kind, n = fills[i - SLOTS]
                wait(eng, s_max if kind == "pass1" else s_exp, n + 1)
            return i % SLOTS

        def wait_filled(eng, stage):
            wait(eng, s_fill, misc_no[stage] + 1)

        def wait_low(eng, j):
            if j >= 0:
                i, k = divmod(j, NK)
                if k == POOL_CHUNK:
                    eng.wait_ge(s_hlo_pool, i + 1)
                else:
                    eng.wait_ge(s_hlo, (NK - 1) * i + k + (k < POOL_CHUNK))

        def adds(i):
            return i - i // E

        def fc1_bank(j):
            return slots[:, (first_bank + j % FC1_SLOTS) % SLOTS, :]

        def fc2_bank(i):
            return acc_bank[:, :] if i % 2 == 0 else slots[:, (first_bank + FC1_SLOTS) % SLOTS, :]

        block = ctx.enter_context(nc.Block())

        def walk(handlers, fills_misc=False):
            for s in schedule:
                if s[0] == "read" and not fills_misc:
                    s = s[1]
                elif s[0] in MISC and not fills_misc:
                    continue
                if s[0] in handlers:
                    handlers[s[0]](*s[1:])

        @block.sync
        def _(sp):
            def load_x(b):
                sp.dma_start(xt[:, NT * b:NT * b + NT, :],
                             x[b].rearrange("(n p) c -> p n c", p=P)).then_inc(s_x[b], 16)

            load_x(0)
            for i, w in enumerate((wqT, wkT, wvT)):
                sp.dma_start(wqkv_s[:, i, :], w).then_inc(s_wqkv, 16)
            for i, v in enumerate((bq, bk)):
                sp.dma_start(bqk_s[:, i:i + 1], v.rearrange("(p a) -> p a", a=1)).then_inc(s_wqkv, 16)
            sp.dma_start(bv_s[:, :], bv.rearrange("(a c) -> a c", a=1).broadcast_to([P, C])).then_inc(s_wqkv, 16)
            load_x(1)
            sp.dma_start(wp_s[:, :], wpT).then_inc(s_wp, 16)
            sp.dma_start(bp_s[:, :], bp.rearrange("(a c) -> a c", a=1).broadcast_to([P, C])).then_inc(s_wp, 16)
            sp.dma_start(w1_s[:, :, :], w1.rearrange("e h f -> h e f")).then_inc(s_w1, 16)
            sp.dma_start(lnw_s[:, :], lnwT).then_inc(s_small, 16)
            sp.dma_start(lnb_s[:, :], lnbT).then_inc(s_small, 16)
            sp.dma_start(b1_s[:, :], b1T).then_inc(s_small, 16)
            sp.dma_start(wg_s[:, :], wg).then_inc(s_small, 16)
            sp.dma_start(b2_s[:, :], b2T).then_inc(s_small, 16)
            sp.dma_start(alpha_s[:, :], alpha.rearrange("(a c) -> a c", a=1).broadcast_to([P, E]))\
              .then_inc(s_small, 16)

            def stack_up(b, i, part):
                wait(sp, s_split, split_no[("split", b, i, PART_STEP[part])] + 1)
                wait(sp, s_zero[b % 2], 16 * 2 if b % 2 else i + 1)
                wait(sp, s_pass2, (b - 1) * NG * UNITS)
                for product in range(PRODUCTS):
                    if STACKED[i][product] == part:
                        r = product * D
                        sp.dma_start(stack[i][b % 2][r:r + D, :, :], parts[:, i, part, :])\
                          .then_inc(s_stack[i][b % 2], 16)
                if (b, i, part) == (0, 1, PARTS - 1):
                    sp.dma_start(w2_s[:, :, :].rearrange("p e (k c) -> p (e k) c", c=C),
                                 w2.rearrange("e (k p) h -> p (e k) h", p=P)).then_inc(s_w2, 16)
                    for later in range(2, B):
                        load_x(later)

            def init_second():
                sp.wait_ge(s_zero[0], 2)
                for i in range(2):
                    sp.dma_start(stack[i][1][PRODUCTS * D:MAX_ROW, :, :], stack[i][0][PRODUCTS * D:MAX_ROW, :, :])\
                      .then_inc(s_zero[1], 16)
                sp.wait_ge(s_minus[0], 1)
                sp.dma_start(stack[1][1][MAX_ROW:K2, :, :], stack[1][0][MAX_ROW:K2, :, :]).then_inc(s_minus[1], 16)

            def store_max(g):
                b, hg = divmod(g, NG)
                wait(sp, s_free, misc_no[("maxT", g)] + 1)
                sp.dma_start(stack[0][b % 2][MAX_ROW:K2, HPG * hg:HPG * hg + HPG, :], max_rows[:, g % 2, :])\
                  .then_inc(s_mrow[g % 2], 16)

            def store_o(g):
                b, hg = divmod(g, NG)
                wait(sp, s_pvout, g + 1)
                sp.dma_start(o_dram[b, hg], oT[:, g % 2, :]).then_inc(s_ostore[g % 2], 16)

            def load_o(b):
                for j in range(2):
                    sp.wait_ge(s_ostore[j], 16 * (b + 1) * NG // 2)
                if b > 0:
                    wait_filled(sp, ("proj", b - 1))
                rows = o_dram[b].rearrange("g (h r) t -> g h r t", h=HPG)
                sp.dma_start(onT[:, :], rows[:, :, 0:D, :]).then_inc(s_oload, 16)
                sp.dma_start(sums[:, :], rows[:, :, D, :].rearrange("g h (a t) -> g h a t", t=H * T // P))\
                  .then_inc(s_sums, 16)

            def store_inverse(b):
                wait(sp, s_inv, b + 1)
                sp.dma_start(inv_dram[b].rearrange("h (a t) -> (h a) t", t=H * T // P), sums[:, :])\
                  .then_inc(s_invst, 16)

            def spread_inverse(b):
                sp.wait_ge(s_invst, 16 * (b + 1))
                wait(sp, s_on, b)
                sp.dma_start(o_inv[:, :], inv_dram[b].rearrange("h (a t) -> h a t", a=1).broadcast_to([H, D, T]))\
                  .then_inc(s_invload, 16)

            def store_comb(b):
                wait(sp, s_free, misc_no[("combT", b)] + 1)
                sp.dma_start(comb_dram[b], combT[:, :]).then_inc(s_combst, 16)

            def load_gates(i):
                b, e = divmod(i, E)
                if i == 0:
                    wait(sp, s_pv, G * NT)
                if e == 0:
                    wait(sp, s_combst, 16 * (b + 1))
                wait(sp, s_scaled, i + 1 - GATE_RING)
                sp.dma_start(gate_rows[:, i % GATE_RING, :], comb_dram[b, e:e + 1, :].broadcast_to([P, T]))\
                  .then_inc(s_gate[i % GATE_RING], 16)

            def store(b):
                wait(sp, s_done, b + 1)
                sp.dma_start(out[b].rearrange("(n p) c -> p n c", p=P),
                             xt[:, NT * b:NT * b + NT, :]).then_inc(s_out, 16)

            walk({"stack": stack_up, "init_second": init_second, "maxT": store_max, "o_store": store_o,
                  "o_load": load_o, "o_invert": store_inverse, "o_spread": spread_inverse, "combT": store_comb,
                  "gates": load_gates, "outT": store})
            sp.wait_ge(s_out, 16 * B)

        @block.tensor
        def _(pe):
            def claim(stage):
                wait(pe, s_free, misc_no[stage])

            def transpose_tiles(stage, src):
                for n in range(NT):
                    mm = pe.transpose(misc[:, n * P:n * P + P], src[:, n, :], ident[:, :])
                mm.then_inc(s_fill, 1)

            def turn_xn(b):
                claim(("xnT", b))
                if b == 0:
                    pe.wait_ge(s_ident, 1)
                wait(pe, s_xn, b + 1)
                transpose_tiles(("xnT", b), xn)

            def project(b, i, name):
                claim((name, b))
                pe.wait_ge(s_wqkv, 16 * 6)
                pe.matmul(misc[:, :], wqkv_s[:, i, :], xnT[:, :], start=True, stop=True).then_inc(s_fill, 1)

            def project_v(b):
                claim(("v", b))
                for n in range(NT):
                    mm = pe.matmul(misc[:, n * P:n * P + P], xnT[:, n * P:n * P + P], wqkv_s[:, 2, :],
                                   start=True, stop=True)
                mm.then_inc(s_fill, 1)

            def pass1(n):
                g, u, w, heads = unit_of(n)
                b, hg = divmod(g, NG)
                slot = wait_slot(pe, ("pass1", n))
                if n % (NG * UNITS) == 0:
                    for i in range(2):
                        pe.wait_ge(s_stack[i][b % 2], 16 * PRODUCTS * (b // 2 + 1))
                cols = columns(n, slot)
                blk = w // P - 1
                q, k = stack[0][b % 2], stack[1][b % 2]
                pe.matmul(cols[:, :, w - P:w], ident_b[:, :], causal[:, 0:len(heads), :],
                          start=True, stop=False, skip_group_check=True)
                for i, h in enumerate(heads):
                    hh = HPG * hg + h
                    mm = pe.matmul(cols[:, i, :], q[0:K1, hh, blk * P:blk * P + P], k[0:K1, hh, 0:w],
                                   start=False, stop=True, skip_group_check=True)
                mm.then_inc(s_pass1, 1)

            def pass2(n):
                g, u, w, heads = unit_of(n)
                b, hg = divmod(g, NG)
                slot = wait_slot(pe, ("pass2", n))
                if n % (NG * UNITS) == 0 and b < 2:
                    pe.wait_ge(s_minus[b], 16 if b else 1)
                if u == 0:
                    pe.wait_ge(s_mrow[g % 2], 16 * (g // 2 + 1))
                cols = columns(n, slot)
                blk = NT - w // P
                q, k = stack[0][b % 2], stack[1][b % 2]
                for i, h in enumerate(heads):
                    hh = HPG * hg + h
                    mm = pe.matmul(cols[:, i, :], k[0:K2, hh, blk * P:blk * P + P], q[0:K2, hh, blk * P:T],
                                   start=True, stop=True)
                mm.then_inc(s_pass2, 1)

            def pv(g, row):
                b, hg = divmod(g, NG)
                last = g * UNITS + ROW_END[row]
                wait(pe, s_cut, last + 1)
                if row == 0:
                    wait(pe, s_pvout, g)
                    wait(pe, s_free, misc_no[("v", b)] + 1)
                for h in range(HPG):
                    u = next(u for u in range(UNITS) if UNIT[u][0] == NT - row and h in UNIT[u][1])
                    p = probs_of(g * UNITS + u)[:, h - UNIT[u][1][0], :]
                    mm = pe.matmul(acc_bank[32 * h:32 * h + 32, row * P:T], v1[:, b % 2, row, HPG * hg + h, :],
                                   p, start=(row == 0), stop=(row == PV_ORDER[-1]), tile_position=(0, 32 * h))
                mm.then_inc(s_pv, 1)

            def turn_max(g):
                claim(("maxT", g))
                wait(pe, s_mpart, 4 * (g + 1))
                pe.transpose(misc[:, :].bitcast(BF16)[0:PARTS * NT * HPG, 0:P],
                             max_parts[:, :, :].rearrange("p a m -> p (a m)"), ident_b[:, :]).then_inc(s_fill, 1)

            def project_out(b):
                claim(("proj", b))
                wait(pe, s_on, b + 1)
                pe.wait_ge(s_wp, 32)
                for n in range(NT):
                    mm = pe.matmul(misc[:, n * P:n * P + P], onT[:, n * P:n * P + P], wp_s[:, :],
                                   start=True, stop=True)
                mm.then_inc(s_fill, 1)

            def hidden_bias(pair):
                claim(("hidden_bias", pair))
                pe.wait_ge(s_w1, 16)
                pe.wait_ge(s_small, 16 * 6)
                for e in range(2 * pair, 2 * pair + 2):
                    for k in range(NK):
                        i = e * NK + k
                        mm = pe.matmul(misc[:, i:i + 1], w1_s[:, e, k * P:k * P + P], lnb_s[:, e:e + 1],
                                       start=True, stop=True)
                mm.then_inc(s_fill, 1)

            def turn_xf(b):
                claim(("xfT", b))
                wait(pe, s_xf, b + 1)
                transpose_tiles(("xfT", b), xf)

            def turn_z(b):
                claim(("zT", b))
                wait(pe, s_z, b + 1)
                transpose_tiles(("zT", b), z)

            def gate(b):
                claim(("gate", b))
                for n in range(NT):
                    mm = pe.matmul(misc[:, n * E:n * E + E], xfT[:, n * P:n * P + P], wg_s[:, :],
                                   start=True, stop=True)
                mm.then_inc(s_fill, 1)

            def turn_comb(b):
                claim(("combT", b))
                wait(pe, s_comb, b + 1)
                for n in range(NT):
                    mm = pe.transpose(misc[0:E, n * P:n * P + P], comb[:, b % 2, n, :], ident[:, :])
                mm.then_inc(s_fill, 1)

            def three_passes(dst, w_hi, w_lo, m_hi, m_lo, first, last):
                pe.matmul(dst, w_hi, m_hi, start=first, stop=False)
                pe.matmul(dst, w_hi, m_lo, start=False, stop=False)
                return pe.matmul(dst, w_lo, m_hi, start=False, stop=last)

            def fc1(i):
                b, e = divmod(i, E)
                if b == 0:
                    wait(pe, s_w1lo, e + 1)
                if e == 0:
                    wait(pe, s_free, misc_no[("zT", b)] + 1)
                w_hi, w_lo = w_parts[0]
                for k in range(NK):
                    j = i * NK + k
                    if j < FC1_SLOTS:
                        wait(pe, s_exp, G * UNITS - SLOTS + j + 1)
                    wait(pe, s_gelu, j + 1 - FC1_SLOTS)
                    three_passes(fc1_bank(j), w_hi[:, e, k * P:k * P + P], w_lo[:, e, k * P:k * P + P],
                                 zT_hi[:, b % 2, :], zT_lo[:, b % 2, :], True, True).then_inc(s_h, 1)

            def fc2(i):
                e = i % E
                if i == 0:
                    wait(pe, s_pvout, G)
                if i < E:
                    wait(pe, s_w2lo, i + 1)
                wait(pe, s_scaled, i - 1)
                w_hi, w_lo = w_parts[1]
                for k in range(NK):
                    wait_low(pe, NK * i + k)
                    mm = three_passes(fc2_bank(i), w_hi[:, e, k * C:k * C + C], w_lo[:, e, k * C:k * C + C],
                                      hidden_hi[:, i % 2, k, :], hidden_lo[:, i % 2, k, :], k == 0, k == NK - 1)
                mm.then_inc(s_y, 1)

            def turn_out(b):
                claim(("outT", b))
                wait(pe, s_sum, adds(E * b + E - 1))
                for n in range(NT):
                    mm = pe.transpose(misc[:, n * P:n * P + P], sumT[:, b % 2, n * P:n * P + P], ident[:, :])
                mm.then_inc(s_fill, 1)

            walk({"xnT": turn_xn, "q": lambda b: project(b, 0, "q"), "k": lambda b: project(b, 1, "k"),
                  "v": project_v, "pass1": pass1, "pass2": pass2, "pv": pv, "maxT": turn_max,
                  "proj": project_out, "hidden_bias": hidden_bias, "xfT": turn_xf,
                  "zT": turn_z, "gate": gate, "combT": turn_comb, "fc1": fc1, "fc2": fc2,
                  "outT": turn_out}, fills_misc=True)

        @block.scalar
        def _(act):
            def copy_misc(stage, dst):
                wait_filled(act, stage)
                act.activation(dst, misc[:, :], ACT.Copy).then_inc(s_free, 1)

            def turn_xn(b):
                copy_misc(("xnT", b), xnT[:, :])

            def biased(b, i, name):
                wait_filled(act, (name, b))
                if b > 0:
                    wait(act, s_split, split_no[("split", b - 1, i, 3)] + 1)
                act.activation(qk32[:, i, :], misc[:, :], ACT.Identity, bias=bqk_s[:, i:i + 1]).then_inc(s_free, 1)

            def split(b, i, step):
                if step == 0 and b > 0:
                    act.wait_ge(s_stack[i][(b - 1) % 2], 16 * PRODUCTS * ((b - 1) // 2 + 1))
                if step == 0:
                    wait(act, s_free, misc_no[(("q", b), ("k", b))[i]] + 1)
                if step % 2 == 0:
                    wait(act, s_split, split_no[("split", b, i, step)])
                    act.activation(parts[:, i, step // 2, :], qk32[:, i, :], ACT.Copy).then_inc(s_split, 1)

            def pass2(n):
                slot = slot_no[("pass2", n)] % SLOTS
                wait(act, s_pass2, n + 1)
                if n >= P_RING:
                    old_g, old_u = divmod(n - P_RING, UNITS)
                    row = NT - UNIT[old_u][0]
                    wait(act, s_pv, NT * old_g + PV_ORDER.index(row) + 1)
                act.activation(probs_of(n), columns(n, slot), ACT.Exp, scale=SCALE).then_inc(s_exp, 1)

            def pv_out(g):
                wait(act, s_pv, NT * (g + 1))
                wait(act, s_ostore[g % 2], 16 * (g // 2))
                act.activation(oT[:, g % 2, :], acc_bank[:, :], ACT.Copy).then_inc(s_pvout, 1)

            def split_w1(e):
                if e == 0:
                    wait(act, s_pass2, (G - NG) * UNITS)
                wait(act, s_w1s, e + 1)
                act.activation(w_parts[0][0][:, e, :], w1_s[:, e, :], ACT.Copy).then_inc(s_w1hi, 1)

            def split_w2(e):
                if e == 0:
                    wait(act, s_pass2, G * UNITS)
                    act.wait_ge(s_w2, 16)
                act.activation(w_parts[1][0][:, e, :], w2_s[:, e, :], ACT.Copy).then_inc(s_w2hi, 1)

            def turn_z(b):
                wait_filled(act, ("zT", b))
                if b >= 2:
                    wait(act, s_h, NK * E * (b - 1))
                act.activation(zT_hi[:, b % 2, :], misc[:, :], ACT.Copy).then_inc(s_zhi, 1)

            def fc1(i):
                b, e = divmod(i, E)
                if i == 0:
                    wait(act, s_pv, G * NT)
                wait(act, s_y, i - 1)
                for k in range(NK):
                    j = i * NK + k
                    wait(act, s_h, j + 1)
                    wait_low(act, j - H_RING)
                    if k % 2 == 0:
                        act.activation(hidden_hi[:, i % 2, k, :], fc1_bank(j), ACT.Gelu_apprx_tanh,
                                       bias=b1_s[:, e * NK + k:e * NK + k + 1])
                    act.activation(hidden[:, j % H_RING, :], fc1_bank(j), ACT.Gelu_apprx_tanh,
                                   bias=b1_s[:, e * NK + k:e * NK + k + 1]).then_inc(s_gelu, 1)

            def turn_comb(b):
                wait_filled(act, ("combT", b))
                wait(act, s_combst, 16 * b)
                act.activation(combT[:, :], misc[0:E, :], ACT.Copy).then_inc(s_free, 1)

            walk({"xnT": turn_xn, "q": lambda b: biased(b, 0, "q"), "k": lambda b: biased(b, 1, "k"),
                  "split": split, "pass2": pass2, "pv_out": pv_out,
                  "xfT": lambda b: copy_misc(("xfT", b), xfT[:, :]),
                  "zT": turn_z, "split_w1": split_w1, "split_w2": split_w2,
                  "combT": turn_comb, "fc1": fc1})

        @block.vector
        def _(dve):
            chain = [0]

            def link(ins):
                ins.then_inc(s_ln, 1)
                chain[0] += 1
                dve.wait_ge(s_ln, chain[0])

            stats_no, variance_no = [0], [0]

            def variance(src):
                for n in range(NT):
                    last = dve.bn_stats(stats[:, n, :], src[:, n, :])
                last.then_inc(s_stats, 1)
                stats_no[0] += 1

            def aggregate(*_):
                dve.wait_ge(s_stats, stats_no[0])
                for n in range(NT):
                    last = dve.bn_aggr(mean_var[:, n, :], stats[:, n, :])
                link(last)
                dve.tensor_scalar(var_eps[:, :], mean_var[:, :, 1], EPS, None, ALU.add).then_inc(s_var, 1)
                variance_no[0] += 1

            def normalise(dst, src, tiles=range(NT)):
                wait(dve, s_rstd, variance_no[0])
                for n in tiles:
                    last = dve.tensor_scalar(dst[:, n, :], src[:, n, :], mean_var[:, n, 0:1], rstd[:, n:n + 1],
                                             ALU.subtract, ALU.mult)
                return last

            def ln_stats(b):
                dve.wait_ge(s_x[b], 16)
                variance(xt[:, NT * b:NT * b + NT, :])

            def ln_apply(b, n):
                if n == 0 and b > 0:
                    wait_filled(dve, ("xnT", b - 1))
                ins = normalise(xn, xt[:, NT * b:NT * b + NT, :], (n,))
                if n == NT - 1:
                    ins.then_inc(s_xn, 1)

            def split(b, i, step):
                if step % 2 == 1 and b == 0:
                    wait(dve, s_split, split_no[("split", b, i, step)])
                    dst = qk32[:, i, :] if step == 1 else parts[:, i, 2, :]
                    dve.tensor_tensor(dst, qk32[:, i, :], parts[:, i, step // 2, :], ALU.subtract)\
                       .then_inc(s_split, 1)

            def put_v(b):
                wait_filled(dve, ("v", b))
                if b == 0:
                    dve.wait_ge(s_vinit, 1)
                wait(dve, s_pv, (b - 1) * NG * NT)
                dve.tensor_tensor(v1[:, b % 2, :, :, 0:D],
                                  misc[:, :].rearrange("p (n h d) -> p n h d", h=H, d=D),
                                  bv_s[:, :].rearrange("p (a h d) -> p a h d", a=1, h=H)
                                  .broadcast_to([P, NT, H, D]), ALU.add).then_inc(s_free, 1)

            def pass1(n):
                g, u, w, heads = unit_of(n)
                slot = slot_no[("pass1", n)] % SLOTS
                wait(dve, s_pass1, n + 1)
                if u == 0 and g >= 2:
                    wait(dve, s_mpart, 4 * (g - 1))
                dve.tensor_reduce(row_max[:, g % 2, heads[0]:heads[-1] + 1, w // P - 1], columns(n, slot),
                                  AX.X, ALU.max)\
                   .then_inc(s_max, 1)

            def turn_max(g):
                wait_filled(dve, ("maxT", g))
                if g >= 2:
                    dve.wait_ge(s_mrow[g % 2], 16 * (g // 2))
                dve.tensor_copy(max_rows[:, g % 2, :], misc[:, :].bitcast(BF16)[0:PARTS * NT * HPG, 0:P])\
                   .then_inc(s_free, 1)

            def invert(b):
                wait(dve, s_sums, 16 * (b + 1))
                dve.reciprocal(sums[:, :], sums[:, :]).then_inc(s_inv, 1)

            def scale_o(b):
                wait(dve, s_oload, 16 * (b + 1))
                wait(dve, s_invload, 16 * (b + 1))
                dve.tensor_tensor(onT[:, :], onT[:, :], o_inv[:, :], ALU.mult).then_inc(s_on, 1)

            def project_out(b):
                wait_filled(dve, ("proj", b))
                wait(dve, s_resid, b + 1)
                tile = xt[:, NT * b:NT * b + NT, :]
                dve.tensor_tensor(tile, misc[:, :].rearrange("p (n c) -> p n c", c=C), tile, ALU.add)\
                   .then_inc(s_free, 1)

            def hidden_bias(pair):
                wait_filled(dve, ("hidden_bias", pair))
                cols = slice(2 * NK * pair, 2 * NK * (pair + 1))
                dve.tensor_tensor(b1_s[:, cols], misc[:, cols], b1_s[:, cols], ALU.add).then_inc(s_free, 1)

            def scale_w1(e):
                wait(dve, s_free, misc_no[("hidden_bias", e // 2)] + 1)
                dve.tensor_scalar(w1_s[:, e, :], w1_s[:, e, :], lnw_s[:, e:e + 1], None, ALU.mult)\
                   .then_inc(s_w1s, 1)

            def stats1(b):
                wait(dve, s_free, misc_no[("proj", b)] + 1)
                variance(xt[:, NT * b:NT * b + NT, :])

            def make_xf(b):
                if b > 0:
                    wait_filled(dve, ("xfT", b - 1))
                normalise(xf, xt[:, NT * b:NT * b + NT, :]).then_inc(s_xf, 1)

            def stats2(b):
                dve.wait_ge(s_xf, b + 1)
                variance(xf)

            def make_z(b):
                if b > 0:
                    wait_filled(dve, ("zT", b - 1))
                normalise(z, xf).then_inc(s_z, 1)

            def gate(b):
                wait_filled(dve, ("gate", b))
                dve.tensor_copy(gate_in[:, :, :], misc[:, 0:NT * E].rearrange("p (n e) -> p n e", e=E))\
                   .then_inc(s_free, 1)

            def top_two(b):
                wait(dve, s_free, misc_no[("gate", b)] + 1)
                for n in range(NT):
                    last = dve.max(top[:, n, :], gate_in[:, n, :])
                link(last)
                for n in range(NT):
                    last = dve.max_index(top_at[:, n, :], top[:, n, :], gate_in[:, n, :])
                link(last)
                if b == 0:
                    dve.wait_ge(s_ids, 1)
                wait(dve, s_second, b)
                dve.tensor_tensor(diff[:, :], top[:, :, 1], top[:, :, 0], ALU.subtract).then_inc(s_diff, 1)
                link(dve.tensor_copy(top_atf[:, :, :], top_at[:, :, 0:2]))
                for j in range(2):
                    last = dve.tensor_tensor(pick[:, j, :, :], expert_ids[:, :, :],
                                             top_atf[:, :, j:j + 1].broadcast_to([P, NT, E]), ALU.is_equal)
                link(last)

            def combine(b):
                wait(dve, s_second, b + 1)
                link(dve.tensor_scalar(denom[:, :], second[:, :], 1.0, None, ALU.add))
                link(dve.reciprocal(gates[:, :, 0], denom[:, :]))
                link(dve.tensor_tensor(gates[:, :, 1], gates[:, :, 0], second[:, :], ALU.mult))
                for j in range(2):
                    last = dve.tensor_tensor(pick[:, j, :, :], pick[:, j, :, :],
                                             gates[:, :, j:j + 1].broadcast_to([P, NT, E]), ALU.mult)
                link(last)
                link(dve.tensor_tensor(pick[:, 0, :, :], pick[:, 0, :, :], pick[:, 1, :, :], ALU.add))
                dve.tensor_tensor(comb[:, b % 2, :, :], pick[:, 0, :, :],
                                  alpha_s[:, :].rearrange("p (a e) -> p a e", a=1).broadcast_to([P, NT, E]),
                                  ALU.mult).then_inc(s_comb, 1)

            def turn_z(b):
                wait(dve, s_zhi, b + 1)
                dve.tensor_tensor(zT_lo[:, b % 2, :], misc[:, :], zT_hi[:, b % 2, :].bitcast(F32), ALU.subtract)\
                   .then_inc(s_free, 1)

            def fc1(i):
                wait(dve, s_y, i - 1)
                for k in range(NK):
                    if k == POOL_CHUNK:
                        continue
                    j = i * NK + k
                    wait(dve, s_gelu, j + 1)
                    if k % 2 == 1:
                        dve.tensor_copy(hidden_hi[:, i % 2, k, :], hidden[:, j % H_RING, :]).then_inc(s_hhi, 1)
                        dve.wait_ge(s_hhi, (j + 1) // 2)
                    dve.tensor_tensor(hidden_lo[:, i % 2, k, :], hidden[:, j % H_RING, :],
                                      hidden_hi[:, i % 2, k, :].bitcast(F32), ALU.subtract).then_inc(s_hlo, 1)

            def fc2(i):
                b, e = divmod(i, E)
                wait(dve, s_y, i + 1)
                dve.wait_ge(s_gate[i % GATE_RING], 16 * (i // GATE_RING + 1))
                if e == 0:
                    dst = sumT[:, b % 2, :]
                    if b >= 2:
                        wait_filled(dve, ("outT", b - 2))
                else:
                    dst = scaled[:, i % 2, :]
                    wait(dve, s_sum, adds(i - 2))
                dve.scalar_tensor_tensor(dst, fc2_bank(i), b2_s[:, e:e + 1], gate_rows[:, i % GATE_RING, :],
                                         ALU.add, ALU.mult).then_inc(s_scaled, 1)
                if i == B * E - 1:
                    dve.wait_ge(s_scaled, i + 1)
                    dve.wait_ge(s_sum, adds(i - 1))
                    dve.tensor_tensor(sumT[:, b % 2, :], sumT[:, b % 2, :], dst, ALU.add).then_inc(s_sum, 1)

            def turn_out(b):
                wait_filled(dve, ("outT", b))
                tile = xt[:, NT * b:NT * b + NT, :]
                dve.tensor_tensor(tile, misc[:, :].rearrange("p (n c) -> p n c", c=C), tile, ALU.add)\
                   .then_inc(s_done, 1)
                dve.sem_inc(s_free, 1)

            walk({"ln_stats": ln_stats, "ln_agg": aggregate, "ln_apply": ln_apply, "split": split, "v": put_v,
                  "pass1": pass1, "maxT": turn_max, "o_invert": invert, "o_scale": scale_o, "proj": project_out,
                  "hidden_bias": hidden_bias, "scale_w1": scale_w1,
                  "r_stats1": stats1, "r_agg1": aggregate, "r_xf": make_xf, "r_stats2": stats2,
                  "r_agg2": aggregate, "r_z": make_z, "zT": turn_z, "gate": gate, "r_top": top_two,
                  "r_comb": combine, "fc1": fc1, "fc2": fc2, "outT": turn_out})

        @block.gpsimd
        def _(pool):
            steps = [0]

            def link(ins):
                ins.then_inc(s_pool, 1)
                steps[0] += 1
                pool.wait_ge(s_pool, steps[0])

            link(pool.memset(minus_half[:, :], -0.5))
            link(pool.memset(euler[:, :], math.e))
            link(pool.memset(ident[:, :], 0.0))
            link(pool.affine_select(out=ident[:, :], in_=ident[:, :], compare_op=ALU.not_equal, fill=1.0,
                                    base=0, pattern=[[-1, P]], channel_multiplier=1))
            link(pool.tensor_copy(ident_b[:, :], ident[:, :]))
            link(pool.memset(causal[:, :, :], 0.0))
            pool.affine_select(out=causal[:, :, :], in_=causal[:, :, :], compare_op=ALU.is_ge, fill=NEG,
                               base=0, pattern=[[0, HPG], [-1, P]], channel_multiplier=1).then_inc(s_ident, 1)
            variance_no = [0]

            def rsqrt(*_):
                variance_no[0] += 1
                wait(pool, s_var, variance_no[0])
                pool.tensor_tensor(rstd[:, :], var_eps[:, :], minus_half[:, :], ALU.pow).then_inc(s_rstd, 1)

            def second_gate(b):
                wait(pool, s_diff, b + 1)
                pool.tensor_tensor(second[:, :], euler[:, :], diff[:, :], ALU.pow).then_inc(s_second, 1)

            def init_v(*_):
                link(pool.memset(v1[:, :, :, :, :].rearrange("p i n h d -> p (i n h) d"), 0.0))
                pool.memset(v1[:, :, :, :, D:D + 1].rearrange("p i n h d -> p (i n h) d"), 1.0).then_inc(s_vinit, 1)
                pool.wait_ge(s_vinit, 1)

            def init_zeros():
                pool.wait_ge(s_rstd, variance_no[0])
                for i in range(2):
                    pool.memset(stack[i][0][0:MAX_ROW, :, :].bitcast(F32), 0.0).then_inc(s_zero[0], 1)
                    pool.wait_ge(s_zero[0], i + 1)

            def init_ones():
                minus_ones = float(np.array([0xBF80BF80], np.uint32).view(np.float32)[0])
                pool.wait_ge(s_rstd, variance_no[0])
                pool.memset(stack[1][0][MAX_ROW:K2, :, :].bitcast(F32), minus_ones).then_inc(s_minus[0], 1)
                pool.wait_ge(s_minus[0], 1)

            def init_experts():
                link(pool.iota(expert_idi[:, :, :], pattern=[[0, NT], [1, E]], base=0, channel_multiplier=0))
                pool.tensor_copy(expert_ids[:, :, :], expert_idi[:, :, :]).then_inc(s_ids, 1)

            def split(b, i, step):
                if step % 2 == 1 and b > 0:
                    wait(pool, s_split, split_no[("split", b, i, step)])
                    dst = qk32[:, i, :] if step == 1 else parts[:, i, 2, :]
                    pool.tensor_tensor(dst, qk32[:, i, :], parts[:, i, step // 2, :], ALU.subtract)\
                        .then_inc(s_split, 1)

            def pass2(n):
                g, u, w, heads = unit_of(n)
                wait(pool, s_exp, n + 1)
                diag = probs_of(n)[:, :, 0:P]
                pool.affine_select(out=diag, in_=diag, compare_op=ALU.is_ge, fill=0.0, base=0,
                                   pattern=[[0, len(heads)], [1, P]], channel_multiplier=-1).then_inc(s_cut, 1)

            def split_max(g):
                wait(pool, s_max, UNITS * (g + 1))
                if g > 0:
                    wait_filled(pool, ("maxT", g - 1))
                source = row_max[:, g % 2, :, :].rearrange("p h n -> p (h n)")
                for step in range(4):
                    part = max_parts[:, (step + 1) // 2, :]
                    if step % 2 == 0:
                        ins = pool.tensor_copy(part, source)
                    else:
                        dst = source if step == 1 else part
                        ins = pool.tensor_tensor(dst, source, max_parts[:, step // 2, :], ALU.subtract)
                    ins.then_inc(s_mpart, 1)
                    pool.wait_ge(s_mpart, 4 * g + step + 1)

            def residual(b):
                wait(pool, s_xn, b + 1)
                pool.wait_ge(s_wp, 32)
                tile = xt[:, NT * b:NT * b + NT, :]
                pool.tensor_tensor(tile, tile, bp_s[:, :].rearrange("p (a c) -> p a c", a=1)
                                   .broadcast_to([P, NT, C]), ALU.add).then_inc(s_resid, 1)

            def low_w(e, i, source, high, low):
                wait(pool, high, e + 1)
                pool.tensor_tensor(w_parts[i][1][:, e, :], source[:, e, :], w_parts[i][0][:, e, :].bitcast(F32),
                                   ALU.subtract).then_inc(low, 1)

            def split_w1(e):
                low_w(e, 0, w1_s, s_w1hi, s_w1lo)

            def split_w2(e):
                low_w(e, 1, w2_s, s_w2hi, s_w2lo)

            def fc1(i):
                wait(pool, s_y, i - 1)
                j = i * NK + POOL_CHUNK
                wait(pool, s_gelu, j + 1)
                pool.tensor_tensor(hidden_lo[:, i % 2, POOL_CHUNK, :], hidden[:, j % H_RING, :],
                                   hidden_hi[:, i % 2, POOL_CHUNK, :].bitcast(F32), ALU.subtract)\
                    .then_inc(s_hlo_pool, 1)

            def fc2(i):
                b, e = divmod(i, E)
                if e > 0 and i < B * E - 1:
                    wait(pool, s_scaled, i + 1)
                    wait(pool, s_sum, adds(i - 1))
                    pool.tensor_tensor(sumT[:, b % 2, :], sumT[:, b % 2, :], scaled[:, i % 2, :], ALU.add)\
                        .then_inc(s_sum, 1)

            walk({"init_v": init_v, "init_zeros": init_zeros, "init_ones": init_ones, "init_experts": init_experts,
                  "ln_agg": rsqrt, "r_agg1": rsqrt, "r_agg2": rsqrt, "split": split, "max_parts": split_max,
                  "pass2": pass2, "residual": residual, "r_exp": second_gate,
                  "split_w1": split_w1, "split_w2": split_w2, "fc1": fc1, "fc2": fc2})


NAMES = ("x", "wqT", "wkT", "wvT", "bq", "bk", "bv", "wpT", "bp", "wg", "alpha", "lnwT", "lnbT",
         "w1", "b1T", "w2", "b2T")


def kernel(L0_attn_x, L0_attn_W_qkv, L0_attn_b_qkv, L0_attn_W_proj, L0_attn_b_proj, L0_ffn_Wg, L0_ffn_alpha,
           L0_ffn_ln_w, L0_ffn_ln_b, L0_ffn_fc1_w, L0_ffn_fc1_b, L0_ffn_fc2_w, L0_ffn_fc2_b):
    import numpy as _np
    import concourse.bacc as _bacc
    from concourse import mybir as _mybir
    from concourse.bass_utils import run_bass_kernel_spmd as _run

    w_qkv, b_qkv = _np.asarray(L0_attn_W_qkv), _np.asarray(L0_attn_b_qkv)
    C = w_qkv.shape[1]
    E, F = _np.shape(L0_ffn_fc1_b)
    b1 = _np.asarray(L0_ffn_fc1_b).reshape(E, F // C, C).transpose(2, 0, 1).reshape(C, E * (F // C))
    wq, wk = (w_qkv[i * C:i * C + C].reshape(16, C // 16, C).transpose(1, 0, 2).reshape(C, C) for i in range(2))
    bq, bk = (b_qkv[i * C:i * C + C].reshape(16, C // 16).T.reshape(C) for i in range(2))
    values = (
        L0_attn_x, wq.T, wk.T, w_qkv[2 * C:3 * C].T, bq, bk, b_qkv[2 * C:3 * C],
        _np.asarray(L0_attn_W_proj).T, L0_attn_b_proj, L0_ffn_Wg, L0_ffn_alpha,
        _np.asarray(L0_ffn_ln_w).T, _np.asarray(L0_ffn_ln_b).T, L0_ffn_fc1_w, b1, L0_ffn_fc2_w,
        _np.asarray(L0_ffn_fc2_b).T,
    )
    nc = _bacc.Bacc("TRN2", target_bir_lowering=False, num_devices=1)
    arrays, args = {}, []
    for name, value in zip(NAMES, values):
        a = _np.ascontiguousarray(value)
        arrays[f"in_{name}"] = a
        args.append(nc.dram_tensor(f"in_{name}", a.shape, _mybir.dt.from_np(a.dtype), kind="ExternalInput").ap())
    out = nc.dram_tensor("out", arrays["in_x"].shape, _mybir.dt.float32, kind="ExternalOutput").ap()
    build(nc, *args, out)
    r = _run(nc, [arrays], core_ids=[0])
    return r.results[0]["out"]
```
